# Optimizing a Trainium2 kernel written in Bass

```python
import numpy as np
import jax
import jax.numpy as jnp

def _softmax(x, axis=-1):
    return jax.nn.softmax(x, axis=axis)

def _gelu(x):
    return jax.nn.gelu(x, approximate=True)

def _silu(x):
    return jax.nn.silu(x)

def _sigmoid(x):
    return jax.nn.sigmoid(x)

def _layernorm(x, axis=-1, eps=1e-05):
    m = jnp.mean(x, axis=axis, keepdims=True)
    v = jnp.var(x, axis=axis, keepdims=True)
    return (x - m) / jnp.sqrt(v + eps)

def _scatter_add(tgt, idx, src, axis=0):
    return tgt.at[idx].add(src)

def _segment_sum(src, seg, n):
    return jax.ops.segment_sum(src, seg, n)
kernel_name = 'mk_adj_resnorm_d4_adj_r2_6f5c56'

def setup_inputs(seed: int=0):
    np.random.seed(seed)
    _w = jnp.asarray

    def _rec_inputs():
        import jax
        import jax.numpy as jnp
        _gk = jax.random.key(seed)
        x = -2.104e-05 + 0.9999 * jax.random.normal(jax.random.fold_in(_gk, 1), (16, 512, 128), jnp.float32)
        _a = jax.random.bernoulli(jax.random.fold_in(_gk, 2), 0.03125, (512, 512))
        _a = jnp.logical_or(_a, jnp.swapaxes(_a, -1, -2))
        _a = jnp.logical_or(_a, jnp.eye(512, dtype=bool))
        _af = _a.astype(jnp.float32)
        _af = _af / jnp.maximum(_af.sum(-1, keepdims=True), 1.0)
        adj = _af
        return (x, adj)
    x, adj = _rec_inputs()

    def _L0_gnn_setup():
        import jax, jax.numpy as jnp
        import numpy as np
        N = 3445
        B = 32
        IN_DIM = 128
        HID_DIM = 128

        def _make_adj(key):
            a = jax.random.uniform(key, (N, N), dtype=jnp.float32)
            a = (a < 0.001).astype(jnp.float32)
            a = jnp.maximum(a, a.T)
            deg = jnp.sum(a, axis=1, keepdims=True)
            return a / jnp.maximum(deg, 1.0)

        def _graph_conv(x, adj, w_loop, w_neigh, b):
            loop = jnp.einsum('bnd,dh->bnh', x, w_loop)
            neigh = jnp.einsum('nm,bmh->bnh', adj, jnp.einsum('bnd,dh->bnh', x, w_neigh))
            return loop + neigh + b
        key = jax.random.key(seed)
        k = jax.random.split(key, 8)
        s1 = 1.0 / np.sqrt(IN_DIM)
        s2 = 1.0 / np.sqrt(HID_DIM)
        return {'x': jax.random.normal(k[0], (B, N, IN_DIM), dtype=jnp.float32), 'adj': _make_adj(k[1]), 'w1_loop': jax.random.normal(k[2], (IN_DIM, HID_DIM), dtype=jnp.float32) * s1, 'w1_neigh': jax.random.normal(k[3], (IN_DIM, HID_DIM), dtype=jnp.float32) * s1, 'b1': jnp.zeros((HID_DIM,), dtype=jnp.float32), 'w2_loop': jax.random.normal(k[4], (HID_DIM, IN_DIM), dtype=jnp.float32) * s2, 'w2_neigh': jax.random.normal(k[5], (HID_DIM, IN_DIM), dtype=jnp.float32) * s2, 'b2': jnp.zeros((IN_DIM,), dtype=jnp.float32)}
    _L0_gnn_all = _L0_gnn_setup()
    _L0_gnn_in = {k: v for k, v in _L0_gnn_all.items() if k in ('w1_loop', 'w1_neigh', 'b1', 'w2_loop', 'w2_neigh', 'b2')}
    del _L0_gnn_all

    def _L1_gnn_setup():
        import jax, jax.numpy as jnp
        import numpy as np
        N_STEPS = 8
        SPATIAL_SCALE = 1.0
        key = jax.random.key(seed)
        ks = jax.random.split(key, 6)
        B, N, D = (32, 512, 128)
        x = jax.random.normal(ks[0], (B, N, D), dtype=jnp.float32)
        adj_mx = jax.random.uniform(ks[1], (N, N), dtype=jnp.float32) / N
        alpha_train = jnp.ones((N,), dtype=jnp.float32)
        w = jnp.eye(D, dtype=jnp.float32) + 0.01 * jax.random.normal(ks[2], (D, D), dtype=jnp.float32)
        d = jax.random.uniform(ks[3], (D,), dtype=jnp.float32)
        fc_in_w = jax.random.normal(ks[4], (D, D), dtype=jnp.float32) * (1.0 / np.sqrt(D))
        fc_in_b = jnp.zeros((D,), dtype=jnp.float32)
        return {'x': x, 'adj_mx': adj_mx, 'alpha_train': alpha_train, 'w': w, 'd': d, 'fc_in_w': fc_in_w, 'fc_in_b': fc_in_b, 'vt': 0}
    _L1_gnn_all = _L1_gnn_setup()
    _L1_gnn_in = {k: v for k, v in _L1_gnn_all.items() if k in ('alpha_train', 'w', 'd', 'fc_in_w', 'fc_in_b')}
    del _L1_gnn_all

    def _L2_gnn_setup():
        import jax, jax.numpy as jnp
        import numpy as np
        B, N, H, OUT, RANK = (64, 512, 128, 128, 10)
        ORDER = 2

        def _conv(x, adj):
            return x * jnp.sum(adj, axis=1)[None, :, None]
        key = jax.random.key(seed)
        ks = jax.random.split(key, 6)
        x = jax.random.normal(ks[0], (B, N, H), dtype=jnp.float32)
        support0 = jax.random.uniform(ks[1], (N, N), dtype=jnp.float32)
        support1 = jax.random.uniform(ks[2], (N, N), dtype=jnp.float32)
        node_vec1 = jax.random.normal(ks[3], (N, RANK), dtype=jnp.float32)
        node_vec2 = jax.random.normal(ks[4], (RANK, N), dtype=jnp.float32)
        d_in = (ORDER * 3 + 1) * H
        W = jax.random.normal(ks[5], (d_in, OUT), dtype=jnp.float32) * (1.0 / np.sqrt(d_in))
        b = jnp.zeros((OUT,), dtype=jnp.float32)
        return {'x': x, 'support0': support0, 'support1': support1, 'node_vec1': node_vec1, 'node_vec2': node_vec2, 'W': W, 'b': b}
    _L2_gnn_all = _L2_gnn_setup()
    _L2_gnn_in = {k: v for k, v in _L2_gnn_all.items() if k in ('node_vec1', 'node_vec2', 'W', 'b')}
    del _L2_gnn_all

    def _L3_gnn_setup():
        import jax, jax.numpy as jnp
        import numpy as np
        BT, N, D, HEADS, E = (512, 64, 128, 4, 256)
        LRELU_SLOPE = 0.2
        EPS = 1e-08
        key = jax.random.key(seed)
        ks = jax.random.split(key, 8)
        d = D
        return {'H': jax.random.normal(ks[0], (BT, N, d), jnp.float32), 'W_lin': jax.random.normal(ks[1], (d, d), jnp.float32) / np.sqrt(d).astype(np.float32), 'W_val': jax.random.normal(ks[2], (d, d), jnp.float32) / np.sqrt(d).astype(np.float32), 'a': jax.random.normal(ks[3], (HEADS, d // HEADS), jnp.float32), 'W_out': jax.random.normal(ks[4], (d, d), jnp.float32) / np.sqrt(d).astype(np.float32), 'A0': jax.random.uniform(ks[5], (N, N), jnp.float32), 'src': jax.random.randint(ks[6], (E,), 0, N, jnp.int32), 'dst': jax.random.randint(ks[7], (E,), 0, N, jnp.int32)}
    _L3_gnn_all = _L3_gnn_setup()
    _L3_gnn_in = {k: v for k, v in _L3_gnn_all.items() if k in ('W_lin', 'W_val', 'a', 'W_out', 'src', 'dst')}
    del _L3_gnn_all
    return {'x': x, 'adj': adj, 'L0_gnn_w1_loop': _L0_gnn_in['w1_loop'], 'L0_gnn_w1_neigh': _L0_gnn_in['w1_neigh'], 'L0_gnn_b1': _L0_gnn_in['b1'], 'L0_gnn_w2_loop': _L0_gnn_in['w2_loop'], 'L0_gnn_w2_neigh': _L0_gnn_in['w2_neigh'], 'L0_gnn_b2': _L0_gnn_in['b2'], 'L1_gnn_alpha_train': _L1_gnn_in['alpha_train'], 'L1_gnn_w': _L1_gnn_in['w'], 'L1_gnn_d': _L1_gnn_in['d'], 'L1_gnn_fc_in_w': _L1_gnn_in['fc_in_w'], 'L1_gnn_fc_in_b': _L1_gnn_in['fc_in_b'], 'L2_gnn_node_vec1': _L2_gnn_in['node_vec1'], 'L2_gnn_node_vec2': _L2_gnn_in['node_vec2'], 'L2_gnn_W': _L2_gnn_in['W'], 'L2_gnn_b': _L2_gnn_in['b'], 'L3_gnn_W_lin': _L3_gnn_in['W_lin'], 'L3_gnn_W_val': _L3_gnn_in['W_val'], 'L3_gnn_a': _L3_gnn_in['a'], 'L3_gnn_W_out': _L3_gnn_in['W_out'], 'L3_gnn_src': _L3_gnn_in['src'], 'L3_gnn_dst': _L3_gnn_in['dst']}

def reference(x, adj, L0_gnn_w1_loop, L0_gnn_w1_neigh, L0_gnn_b1, L0_gnn_w2_loop, L0_gnn_w2_neigh, L0_gnn_b2, L1_gnn_alpha_train, L1_gnn_w, L1_gnn_d, L1_gnn_fc_in_w, L1_gnn_fc_in_b, L2_gnn_node_vec1, L2_gnn_node_vec2, L2_gnn_W, L2_gnn_b, L3_gnn_W_lin, L3_gnn_W_val, L3_gnn_a, L3_gnn_W_out, L3_gnn_src, L3_gnn_dst):
    import jax
    import jax.numpy as jnp

    def _L0_gnn_ref(x, adj, w1_loop, w1_neigh, b1, w2_loop, w2_neigh, b2):
        import jax, jax.numpy as jnp
        import numpy as np
        N = 3445
        B = 32
        IN_DIM = 128
        HID_DIM = 128

        def _make_adj(key):
            a = jax.random.uniform(key, (N, N), dtype=jnp.float32)
            a = (a < 0.001).astype(jnp.float32)
            a = jnp.maximum(a, a.T)
            deg = jnp.sum(a, axis=1, keepdims=True)
            return a / jnp.maximum(deg, 1.0)

        def _graph_conv(x, adj, w_loop, w_neigh, b):
            loop = jnp.einsum('bnd,dh->bnh', x, w_loop)
            neigh = jnp.einsum('nm,bmh->bnh', adj, jnp.einsum('bnd,dh->bnh', x, w_neigh))
            return loop + neigh + b
        h = jax.nn.relu(_graph_conv(x, adj, w1_loop, w1_neigh, b1))
        h = jax.nn.relu(_graph_conv(h, adj, w2_loop, w2_neigh, b2))
        return (x + h) * 0.5

    def _L1_gnn_ref(x, adj_mx, alpha_train, w, d, fc_in_w, fc_in_b, vt):
        import jax, jax.numpy as jnp
        import numpy as np
        N_STEPS = 8
        SPATIAL_SCALE = 1.0
        x0 = jax.lax.stop_gradient(x)
        h = jnp.einsum('bnd,ed->bne', x, fc_in_w) + fc_in_b
        alph = jax.nn.sigmoid(alpha_train)[:, None]
        d_clamped = jnp.clip(d, 0.0, 1.0)
        w_eff = w * d_clamped @ w.T
        dt = jnp.float32(SPATIAL_SCALE / N_STEPS)

        def euler_step(h, _):
            ax = jnp.einsum('nm,bmd->bnd', adj_mx, h)
            f = alph * 0.5 * (ax - h) + h @ w_eff - h + x0
            return (h + dt * f, None)
        h, _ = jax.lax.scan(euler_step, h, None, length=N_STEPS)
        return h

    def _L2_gnn_ref(x, support0, support1, node_vec1, node_vec2, W, b):
        import jax, jax.numpy as jnp
        import numpy as np
        B, N, H, OUT, RANK = (64, 512, 128, 128, 10)
        ORDER = 2

        def _conv(x, adj):
            return x * jnp.sum(adj, axis=1)[None, :, None]
        adaptive = jax.nn.softmax(jax.nn.relu(node_vec1 @ node_vec2), axis=1)
        outputs = [x]
        for adj in (support0, support1, adaptive):
            x1 = _conv(x, adj)
            outputs.append(x1)
            for _ in range(2, ORDER + 1):
                x1 = _conv(x1, adj)
                outputs.append(x1)
        out = jnp.concatenate(outputs, axis=2)
        out = out @ W + b
        return out

    def _L3_gnn_ref(H, W_lin, W_val, a, W_out, A0, src, dst):
        import jax, jax.numpy as jnp
        import numpy as np
        BT, N, D, HEADS, E = (512, 64, 128, 4, 256)
        LRELU_SLOPE = 0.2
        EPS = 1e-08
        bt, n, d = H.shape
        h, dh = a.shape
        Xq = (H @ W_lin.T).reshape(bt, n, h, dh)
        Xv = (H @ W_val.T).reshape(bt, n, h, dh)
        Qs = Xq[:, src]
        Kt = Xq[:, dst]
        e = jnp.einsum('behd,hd->beh', jax.nn.leaky_relu(Qs + Kt, LRELU_SLOPE), a)
        e = e + jnp.log(A0[src, dst] + EPS)[None, :, None]
        e_t = e.transpose(1, 0, 2)
        m = jax.ops.segment_max(e_t, src, num_segments=n)
        ex = jnp.exp(e_t - m[src])
        denom = jax.ops.segment_sum(ex, src, num_segments=n)
        attn = ex / denom[src]
        Vt = Xv[:, dst].transpose(1, 0, 2, 3)
        Y = jax.ops.segment_sum(attn[..., None] * Vt, src, num_segments=n)
        Y = Y.transpose(1, 0, 2, 3).reshape(bt, n, d)
        return Y @ W_out.T
    x = _layernorm(x + _L0_gnn_ref(x, adj, L0_gnn_w1_loop, L0_gnn_w1_neigh, L0_gnn_b1, L0_gnn_w2_loop, L0_gnn_w2_neigh, L0_gnn_b2), axis=-1)
    x = _layernorm(x + _L1_gnn_ref(x, adj, L1_gnn_alpha_train, L1_gnn_w, L1_gnn_d, L1_gnn_fc_in_w, L1_gnn_fc_in_b, 0), axis=-1)
    x = _layernorm(x + _L2_gnn_ref(x, adj, adj, L2_gnn_node_vec1, L2_gnn_node_vec2, L2_gnn_W, L2_gnn_b), axis=-1)
    x = _layernorm(x + _L3_gnn_ref(x, L3_gnn_W_lin, L3_gnn_W_val, L3_gnn_a, L3_gnn_W_out, adj, L3_gnn_src, L3_gnn_dst), axis=-1)
    return x

_drawn_inputs = setup_inputs


def setup_inputs(seed=0):
    import zlib

    import numpy as np

    out = dict(_drawn_inputs(seed))
    spreads = {'L0_gnn_b1': (0.0, 0.374),
     'L0_gnn_b2': (0.0, 0.338),
     'L1_gnn_alpha_train': (1.0, 0.6),
     'L1_gnn_fc_in_b': (0.0, 0.1),
     'L2_gnn_b': (0.0, 0.1)}
    factors = {'L2_gnn_node_vec1': 200.0, 'L2_gnn_node_vec2': 200.0}
    for name, (base, spread) in spreads.items():
        noise = np.random.default_rng([zlib.crc32(name.encode()), seed]).standard_normal(out[name].shape)
        drawn = base * np.exp(spread * noise) if base else spread * noise
        out[name] = jnp.asarray(drawn.astype(out[name].dtype))
    for name, factor in factors.items():
        out[name] = (out[name] * factor).astype(out[name].dtype)
    return out
```

```python
from contextlib import ExitStack
from math import comb

import concourse.bass as bass
from concourse import mybir

F32 = mybir.dt.float32
F32R = mybir.dt.float32r
I32 = mybir.dt.int32
ALU = mybir.AluOpType
ACT = mybir.ActivationFunctionType
AX = mybir.AxisListType.X
AXES = mybir.AxisListType.XY

P = 128
STREAMS = 2
EULER_STEPS = 8
LOT = 3
BIG = 3.0e38


def numbered(order):
    listed = [(what, i) for whats, n in order for i in range(n) for what in whats.split("+")]
    return {step: place + 1 for place, step in enumerate(listed)}


def after(steps, turn, what, i=0):
    return turn * len(steps) + steps[what, i]


def build_program(nc, t, out):
    B, N, D = t["x"].shape
    NB = N // P
    E = t["L3_gnn_src"].shape[0]
    EB = E // P
    HEADS, DH = t["L3_gnn_a"].shape
    RANK = t["L2_gnn_node_vec1"].shape[1]
    GB = 512 // D
    TURNS = B // (GB * STREAMS)
    W = GB * D
    DT = 1.0 / EULER_STEPS
    NQ = EULER_STEPS + 1
    LOTS = NQ // LOT
    HR = GB * HEADS
    assert D == P and W == 512 and NB == 4 and EB == 2 and TURNS * GB * STREAMS == B and NQ % LOT == 0

    ctx = ExitStack()
    with ctx:
        def sb(name, shape, dt=F32):
            return ctx.enter_context(nc.sbuf_tensor(name, shape, dt))

        def sem(name):
            return ctx.enter_context(nc.semaphore(name))

        def raw(ap):
            return ap.bitcast(F32)

        X = [sb(f"X{s}", [P, NB, GB, D]) for s in range(STREAMS)]
        ZH = [sb(f"ZH{s}", [P, NB, GB, D], F32R) for s in range(STREAMS)]
        ZL = [sb(f"ZL{s}", [P, NB, GB, D], F32R) for s in range(STREAMS)]
        TH = [sb(f"TH{s}", [P, GB, N], F32R) for s in range(STREAMS)]
        TL = [sb(f"TL{s}", [P, GB, N], F32R) for s in range(STREAMS)]
        F = [sb(f"F{s}", [P, NB, GB, D]) for s in range(STREAMS)]
        Y = [sb(f"Y{s}", [P, LOT * NB * GB * D]) for s in range(STREAMS)]
        stats = [sb(f"stats{s}", [P, NB * GB, 6]) for s in range(STREAMS)]
        small = [sb(f"small{s}", [P, 8, NB * GB]) for s in range(STREAMS)]

        ident = sb("ident", [P, P])
        ones = sb("ones", [P, P])
        minus_half = sb("minus_half", [P, NB * GB])
        BTH = sb("BTH", [P, NB, N], F32R)
        BTL = sb("BTL", [P, NB, N], F32R)
        r_row = sb("r_row", [P, N])
        w1H = sb("w1H", [P, 2, D], F32R)
        w1L = sb("w1L", [P, 2, D], F32R)
        w2H = sb("w2H", [P, 2 * D], F32R)
        w2L = sb("w2L", [P, 2 * D], F32R)
        b2_row = sb("b2_row", [P, 2, D])
        QH = sb("QH", [P, NQ, D], F32R)
        QL = sb("QL", [P, NQ, D], F32R)
        VH = sb("VH", [P, 5, D], F32R)
        VL = sb("VL", [P, 5, D], F32R)
        gH = sb("gH", [P, 2, D], F32R)
        gL = sb("gL", [P, 2, D], F32R)
        w_out = sb("w_out", [P, D])
        E1 = sb("E1", [P, NB, 2 * E], F32R)
        S1 = sb("S1", [P, EB, N], F32R)
        head_of = sb("head_of", [HR, GB, D])
        a_pad = sb("a_pad", [P, 2 * HR - HEADS])
        edge = sb("edge", [HR, 3, E + 1])
        log_a = sb("log_a", [1, E])
        inexact = sb("inexact", [1, 1], I32)
        cols = sb("cols", [P, 56])
        names = {}

        def col(name, n=1):
            if name not in names:
                names[name] = sum(k for _, k in names.values()), n
            at, k = names[name]
            assert at + k <= 56
            return cols[:, at:at + k]

        r, r_inv, neg_r, row_sum, c_neg, c_r, t_sum, b1 = (
            col(x, n) for x, n in (("r", NB), ("r_inv", NB), ("neg_r", NB), ("row_sum", NB), ("c_neg", NB),
                                   ("c_r", NB), ("t_sum", NB), ("b1", 1)))

        at = [0, 0]

        def scratch(s, shape, parts=P):
            n = 1
            for k in shape:
                n *= k
            lo = at[s]
            at[s] += n
            assert at[s] <= LOT * NB * GB * D, at
            v = Y[s][0:parts, lo:lo + n]
            if len(shape) == 2:
                v = v.rearrange("p (a b) -> p a b", b=shape[1])
            return v

        def flat(tile):
            return tile[:, :, :, :].rearrange("p a b c -> p (a b c)")

        adj_sb = flat(F[1]).rearrange("p (a b) -> p a b", b=N)
        b_hi, b_lo = (flat(z).rearrange("p (a b) -> p a b", b=N) for z in (ZH[1], ZL[1]))
        node_row = scratch(1, [N])
        node_col = scratch(1, [NB])
        ends_row_i = scratch(1, [2 * E]).bitcast(I32)
        ends_col_i = scratch(1, [2 * EB]).bitcast(I32)
        ends_col = scratch(1, [2 * EB])
        key_row = scratch(1, [E])
        key_col = scratch(1, [EB])
        rank = scratch(1, [EB])
        less = scratch(1, [E])
        perm = scratch(1, [EB, E])
        perm_ends = scratch(1, [EB, 2 * E])
        ends_row = scratch(1, [2 * E])
        src_col = scratch(1, [EB])
        one_src = scratch(1, [NB, E])
        picked = scratch(1, [NB, E])
        w_in = scratch(0, [9, D])
        W1N, W1L, W2N, W2L, WE, FC, WLIN, WVAL, WOUT = range(9)
        w_l2 = scratch(0, [7, D])
        w_t = scratch(0, [2, D])
        V = scratch(0, [D])
        nv1 = scratch(0, [NB, RANK])
        nv1_t = scratch(0, [N], RANK)
        nv2 = scratch(0, [N], RANK)
        b_l2 = scratch(0, [D])
        w_sum = scratch(0, [5, D])
        ident_v = scratch(0, [D])
        last_power = scratch(0, [D])
        q_t = scratch(0, [NQ, D])
        chain = flat(F[0]).rearrange("p (a b) -> p a b", b=2 * D)
        soft = flat(F[1])[:, 0:N]
        a_col, d_col, fcb_col, alpha, tmp_a, tmp_b, tmp_c = (
            col(x, n) for x, n in (("a", 1), ("d", 1), ("fcb", 1), ("alpha", NB), ("tmp_a", NB), ("tmp_b", NB),
                                   ("tmp_c", NB)))
        low_col = col("low", 1)

        bank = [[ctx.enter_context(nc.psum_tensor(f"bank{s}_{j}", [P, 512], F32)) for j in range(4)]
                for s in range(STREAMS)]

        LN = [("mean2", 1), ("half_difference", 1), ("m2", 1), ("square", 1), ("spread", 1), ("variance", 1),
              ("mean", 1)]

        def norm(n):
            return [(f"stats{n}", NB * GB)] + [(f"{what}{n}", 1) for what, _ in LN] + [(f"x{n}", NB * GB)]

        lots = [(l, [EULER_STEPS - l * LOT - i for i in range(LOT)]) for l in range(LOTS)]
        pe_order = [("t0", 4), ("neigh1", 4), ("conv1", 4), ("pair2", 8), ("neigh2", 4), ("t1", 4)]
        act_order = [("x0_hi", 4), ("t0_hi", 4), ("neigh1_hi", 4), ("h1+h1_hi", 4), ("x_3", 4), ("z2_hi", 8),
                     ("t1_hi", 4)]
        dve_order = [("t0_lo", 4), ("neigh1", 4), ("z2_lo+loop2", 8), ("conv2", 4), ("y0", 4)] + norm(0) \
            + [("t1_lo", 4)]
        pool_order = [("x0_lo", 4), ("neigh1_lo", 4), ("h1_lo", 4), ("rstd0", 1)]
        for l, ks in lots:
            pe_order.append((f"lot{l}", NB * GB))
            act_order.append((f"lot{l}", NB * GB))
            for k in ks:
                if k < EULER_STEPS:
                    pe_order.append((f"euler{k}", NB))
                    dve_order += [(f"local{k}", NB), (f"euler{k}", NB)]
                if k > 0:
                    act_order.append((f"euler{k}_hi", NB))
                    pool_order.append((f"euler{k}_lo", NB))
        dve_order += norm(1) + [("t2_lo", 4)] + [("l2", 4 * NB)] + norm(2)
        pool_order += [("rstd1", 1), ("rstd2", 1), ("x3_lo", 4), ("rstd3", 1)]
        pe_order += [("t2", 4), ("l2", 2 * NB * GB), ("gather", 4), ("qv", 4), ("score", 1), ("spread", 4),
                     ("wout", 4), ("scatter", 4)]
        act_order += [("t2_hi", 4), ("l2", 2 * NB * GB), ("x3_hi", 4), ("gather_hi", 4), ("q", 4), ("v", 4),
                      ("exp", 1), ("wout_hi", 4)]
        dve_order += [("gather_lo", 4), ("leaky", 4), ("seg", 7), ("mix", 4), ("wout_lo", 4), ("y3", 4)] + norm(3)

        pe_steps = numbered(pe_order)
        pe_done = [sem(f"pe_done{s}") for s in range(STREAMS)]
        act_steps = numbered(act_order)
        act_done = [sem(f"act_done{s}") for s in range(STREAMS)]
        dve_steps = numbered(dve_order)
        dve_done = [sem(f"dve_done{s}") for s in range(STREAMS)]
        pool_steps = numbered(pool_order)
        pool_done = [sem(f"pool_done{s}") for s in range(STREAMS)]
        x_loaded = [sem(f"x_loaded{s}") for s in range(STREAMS)]
        y_stored = [sem(f"y_stored{s}") for s in range(STREAMS)]

        last_reader = {"t0": (dve_done, dve_steps, "t0_lo"), "neigh1": (dve_done, dve_steps, "neigh1"), "conv1": (act_done, act_steps, "h1_hi"),
                       "pair2": (dve_done, dve_steps, "loop2"), "neigh2": (dve_done, dve_steps, "conv2"), "t1": (dve_done, dve_steps, "t1_lo"), "t2": (dve_done, dve_steps, "t2_lo"),
                       "l2": (act_done, act_steps, "l2"), "gather": (dve_done, dve_steps, "gather_lo"), "qv": (act_done, act_steps, "v"), "score": (dve_done, dve_steps, "seg"),
                       "spread": (dve_done, dve_steps, "mix"), "wout": (dve_done, dve_steps, "wout_lo"), "scatter": (dve_done, dve_steps, "y3")}
        for l, ks in lots:
            last_reader[f"lot{l}"] = (act_done, act_steps, f"lot{l}")
            for k in ks:
                last_reader[f"euler{k}"] = (dve_done, dve_steps, f"euler{k}")
        bank_user = {}
        before = {}
        for stage, n in pe_order:
            for i in range(n):
                bank_user[stage, i] = before.get(i % 4)
                before[i % 4] = (stage, i)

        loads = {
            "adj": [(adj_sb, t["adj"].rearrange("(a p) m -> p a m", p=P))],
            "w": [(w_in[:, W1N, :], t["L0_gnn_w1_neigh"]), (w_in[:, W1L, :], t["L0_gnn_w1_loop"]),
                  (w_in[:, W2N, :], t["L0_gnn_w2_neigh"]), (w_in[:, W2L, :], t["L0_gnn_w2_loop"]),
                  (w_in[:, WE, :], t["L1_gnn_w"]), (w_in[:, FC, :], t["L1_gnn_fc_in_w"]),
                  (w_in[:, WLIN, :], t["L3_gnn_W_lin"]), (w_in[:, WVAL, :], t["L3_gnn_W_val"]),
                  (w_in[:, WOUT, :], t["L3_gnn_W_out"]),
                  (w_l2, t["L2_gnn_W"].rearrange("(a p) n -> p a n", p=P)),
                  (b1, t["L0_gnn_b1"].rearrange("(p a) -> p a", a=1)),
                  (fcb_col, t["L1_gnn_fc_in_b"].rearrange("(p a) -> p a", a=1)),
                  (d_col, t["L1_gnn_d"].rearrange("(p a) -> p a", a=1)),
                  (a_col, t["L3_gnn_a"].rearrange("h (d a) -> (h d) a", a=1)),
                  (alpha, t["L1_gnn_alpha_train"].rearrange("(a p) -> p a", p=P)),
                  (b2_row[:, 0, :], t["L0_gnn_b2"].partition_broadcast(P)),
                  (b2_row[:, 1, :], t["L0_gnn_b2"].partition_broadcast(P)),
                  (b_l2, t["L2_gnn_b"].partition_broadcast(P)),
                  (nv1, t["L2_gnn_node_vec1"].rearrange("(a p) k -> p a k", p=P)),
                  (nv2, t["L2_gnn_node_vec2"])],
            "ends": [(ends_row_i[:, 0:E], t["L3_gnn_src"].partition_broadcast(P)),
                     (ends_row_i[:, E:2 * E], t["L3_gnn_dst"].partition_broadcast(P)),
                     (ends_col_i[:, 0:EB], t["L3_gnn_src"].rearrange("(a p) -> p a", p=P)),
                     (ends_col_i[:, EB:2 * EB], t["L3_gnn_dst"].rearrange("(a p) -> p a", p=P))],
        }
        loaded = {what: sem(f"{what}_loaded") for what in loads}
        w_dve_done = sem("w_dve_done")
        w_dve_steps = numbered([("b_split", 1), ("r_diag", 1), ("r_row", 1), ("w_by_d", 1), ("v", 1), ("chain0", 1),
                                        ("nv1_t", 1), ("perm", 1), ("ends_row", 1), ("one_hot", 1), ("l2_sum", 1),
                                        ("power", EULER_STEPS), ("l2_w", 1), ("weights", 1), ("picked", NB),
                                        ("log_in", 1), ("rowmax+t_sum", NB), ("q", 1), ("done", 1)])
        w_act_done = sem("w_act_done")
        w_act_steps = numbered([("sigmoid", 1), ("b_t", 2 * NB), ("w_t", 1), ("log", 1), ("soft", NB),
                                        ("q_t", LOTS)])
        w_pe_done = sem("w_pe_done")
        w_pe_steps = numbered([("b_t", 2 * NB), ("r_row", 1), ("w_t", 1), ("w_eff", 1), ("nv1_t", 1),
                                      ("ends_row", 1), ("src_col", 1), ("power", EULER_STEPS), ("l2_mean", 2),
                                      ("g_t", 1), ("adj_rows", NB), ("picked", 1), ("logits", NB), ("q_t", LOTS)])
        w_pool_done = sem("w_pool_done")
        w_pool_steps = numbered([("const", 1), ("done", 1)])
        psA, psB = bank[0], bank[1]
        q_bank = [psA[0], psA[1], psB[0]]
        pool_chain, dve_chain = sem("pool_chain"), sem("dve_chain")

        rest = perm_ends[:, 0, :]

        def wide(s, a):
            return bank[s][a][:, :].rearrange("p (b d) -> p b d", d=D)

        def y4(s, b):
            return Y[s][:, b * N:(b + 1) * N].rearrange("p (a n) -> p a n", a=NB)

        def z2(z, a):
            return z[:, a, :, :]

        def y_terms(s):
            return Y[s][:, :].rearrange("p (k a b d) -> p k a b d", k=LOT, a=NB, b=GB)

        def state(s, k, a):
            return y_terms(s)[:, 0, a, :, :] if k == EULER_STEPS else F[s][:, a, :, :]

        def half(s, i, part):
            return bank[s][i % 4][:, :].rearrange("p (b w d) -> p b w d", b=2, w=2)[:, :, part, :]

        def terms2(s, a):
            lo = a % 2 * 5 * W
            return Y[s][:, lo:lo + 5 * W].rearrange("p (j b d) -> p j b d", j=5, b=GB)

        def l3(s, kind, b):
            lo = (kind * GB + b) * E
            return Y[s][:, lo:lo + E]

        def seg(s, i):
            lo = 4 * GB * E + i * E
            return Y[s][0:HR, lo:lo + E]

        block = ctx.enter_context(nc.Block())

        @block.sync
        def _(sync):
            for what, copies in loads.items():
                for dst, src in copies:
                    sync.dma_start(dst, src, allow_slow_non_contiguous=True).then_inc(loaded[what], 16)
            x_v = t["x"].rearrange("(g b) (a p) d -> g p a b d", b=GB, p=P)
            out_v = out.rearrange("(g b) (a p) d -> g p a b d", b=GB, p=P)

            def load(s, group):
                for a in range(NB):
                    sync.dma_start(X[s][:, a, :, :], x_v[group, :, a, :, :]).then_inc(x_loaded[s], 16)

            def store(s, turn):
                sync.wait_ge(dve_done[s], after(dve_steps, turn, "x3", NB * GB - 1))
                for a in range(NB):
                    sync.dma_start(out_v[turn * STREAMS + s, :, a, :, :], X[s][:, a, :, :]).then_inc(y_stored[s], 16)

            for s in range(STREAMS):
                load(s, s)
            with sync.Fori(0, TURNS - 1) as turn:
                for s in range(STREAMS):
                    store(s, turn)
                    sync.wait_ge(y_stored[s], (turn + 1) * (16 * NB))
                    load(s, turn * STREAMS + (STREAMS + s))
            for s in range(STREAMS):
                store(s, TURNS - 1)
            for s in range(STREAMS):
                sync.wait_ge(y_stored[s], TURNS * 16 * NB)

        @block.gpsimd
        def _(gp):
            g = nc.gpsimd
            n = 0

            def link(ins):
                nonlocal n
                n += 1
                ins.then_inc(pool_chain, 1)
                gp.wait_ge(pool_chain, n)

            link(g.memset(ident[:, :], 0.0))
            link(g.affine_select(out=ident[:, :], in_=ident[:, :], compare_op=ALU.not_equal, fill=1.0, base=0,
                                 pattern=[[-1, P]], channel_multiplier=1))
            link(g.memset(ones[:, :], 1.0))
            link(g.memset(minus_half[:, :], -0.5))
            link(g.memset(head_of[:, :, :], 0.0))
            link(g.affine_select(out=head_of[:, :, :].rearrange("p b (h d) -> p b h d", h=HEADS),
                                 in_=head_of[:, :, :].rearrange("p b (h d) -> p b h d", h=HEADS),
                                 compare_op=ALU.not_equal, fill=1.0, base=0,
                                 pattern=[[-HEADS, GB], [-1, HEADS], [0, DH]], channel_multiplier=1))
            link(g.iota(node_row, pattern=[[1, N]], base=0, channel_multiplier=0,
                        allow_small_or_imprecise_dtypes=True))
            link(g.iota(node_col, pattern=[[P, NB]], base=0, channel_multiplier=1,
                        allow_small_or_imprecise_dtypes=True))
            g.memset(a_pad[:, :], 0.0).then_inc(w_pool_done, 1)
            gp.wait_ge(w_dve_done, after(w_dve_steps, 0, "done"))
            gp.wait_ge(w_act_done, after(w_act_steps, 0, "q_t", LOTS - 1))
            g.memset(small[0][:, 7, :], 0.0).then_inc(w_pool_done, 1)

            def low_part(turn, s, lo, whole, hi, what, i):
                g.tensor_tensor(lo, whole, raw(hi), ALU.subtract).then_inc(pool_done[s], 1)

            with gp.Fori(0, TURNS) as turn:
                for s in range(STREAMS):
                    gp.wait_ge(x_loaded[s], (turn + 1) * (16 * NB))
                    for a in range(NB):
                        gp.wait_ge(act_done[s], after(act_steps, turn, "x0_hi", a))
                        low_part(turn, s, ZL[s][:, a, :, :], X[s][:, a, :, :], ZH[s][:, a, :, :], "x0_lo", a)
                for s in range(STREAMS):
                    for b in range(GB):
                        gp.wait_ge(act_done[s], after(act_steps, turn, "neigh1_hi", b))
                        low_part(turn, s, ZL[s][:, :, b, :], y4(s, b), ZH[s][:, :, b, :], "neigh1_lo", b)
                for s in range(STREAMS):
                    for b in range(GB):
                        gp.wait_ge(act_done[s], after(act_steps, turn, "h1_hi", b))
                        low_part(turn, s, TL[s][:, b, :], Y[s][:, 2048 + b * N:2048 + (b + 1) * N], TH[s][:, b, :],
                                 "h1_lo", b)

                def rstd(s, n):
                    gp.wait_ge(dve_done[s], after(dve_steps, turn, f"variance{n}"))
                    g.tensor_tensor(small[s][:, 6, :], small[s][:, 5, :], minus_half[:, :], ALU.pow).then_inc(pool_done[s], 1)

                for s in range(STREAMS):
                    rstd(s, 0)
                for k in range(EULER_STEPS, 0, -1):
                    for s in range(STREAMS):
                        for a in range(NB):
                            gp.wait_ge(act_done[s], after(act_steps, turn, f"euler{k}_hi", a))
                            low_part(turn, s, z2(ZL[s], a), state(s, k, a), z2(ZH[s], a), f"euler{k}_lo", a)
                for n in (1, 2):
                    for s in range(STREAMS):
                        rstd(s, n)
                for s in range(STREAMS):
                    for a in range(NB):
                        gp.wait_ge(act_done[s], after(act_steps, turn, "x3_hi", a))
                        low_part(turn, s, ZL[s][:, a, :, :], X[s][:, a, :, :], ZH[s][:, a, :, :], "x3_lo", a)
                for s in range(STREAMS):
                    rstd(s, 3)

        @block.scalar
        def _(ac):
            A = nc.scalar

            def copy(out_, in_, **more):
                return A.activation(out_, in_, ACT.Copy, **more)

            ac.wait_ge(loaded["w"], 16 * len(loads["w"]))
            A.activation(tmp_a, alpha, ACT.Exp, scale=-1.0).then_inc(w_act_done, 1)
            for i in range(2 * NB):
                ac.wait_ge(w_pe_done, after(w_pe_steps, 0, "b_t", i))
                copy((BTH if i < NB else BTL)[:, i % NB, :], psA[i % 4][:, :]).then_inc(w_act_done, 1)
            ac.wait_ge(w_pe_done, after(w_pe_steps, 0, "w_t"))
            copy(w_t[:, 0, :], psA[0][:, 0:D]).then_inc(w_act_done, 1)
            ac.wait_ge(w_dve_done, after(w_dve_steps, 0, "log_in"))
            A.activation(log_a[:, :], log_a[:, :], ACT.Ln).then_inc(w_act_done, 1)
            for a in range(NB):
                ac.wait_ge(w_dve_done, after(w_dve_steps, 0, "rowmax", a))
                A.activation(soft, soft, ACT.Exp, bias=tmp_b[:, a:a + 1], accum_out=tmp_c[:, a:a + 1]).then_inc(w_act_done, 1)
            for i in range(LOTS):
                ac.wait_ge(w_pe_done, after(w_pe_steps, 0, "q_t", i))
                copy(QH[:, i * LOT:(i + 1) * LOT, :], q_bank[i][:, 0:LOT * D]).then_inc(w_act_done, 1)
            ac.wait_ge(w_dve_done, after(w_dve_steps, 0, "done"))

            def from_psum(turn, s, stage, i, what, out_, part=None, j=None, **more):
                ac.wait_ge(pe_done[s], after(pe_steps, turn, stage, i))
                src = bank[s][i % 4][:, :] if part is None else part
                copy(out_, src, **more).then_inc(act_done[s], 1)

            with ac.Fori(0, TURNS) as turn:
                for s in range(STREAMS):
                    ac.wait_ge(x_loaded[s], (turn + 1) * (16 * NB))
                    for a in range(NB):
                        copy(ZH[s][:, a, :, :], X[s][:, a, :, :]).then_inc(act_done[s], 1)
                for s in range(STREAMS):
                    for b in range(GB):
                        from_psum(turn, s, "t0", b, "t0_hi", TH[s][:, b, :])
                for s in range(STREAMS):
                    for b in range(GB):
                        ac.wait_ge(dve_done[s], after(dve_steps, turn, "neigh1", b))
                        copy(ZH[s][:, :, b, :], y4(s, b)).then_inc(act_done[s], 1)
                for s in range(STREAMS):
                    for b in range(GB):
                        ac.wait_ge(pe_done[s], after(pe_steps, turn, "conv1", b))
                        A.activation(Y[s][:, 2048 + b * N:2048 + (b + 1) * N], bank[s][b][:, :],
                                                   ACT.Relu, bias=b1).then_inc(act_done[s], 1)
                        A.activation(TH[s][:, b, :], bank[s][b][:, :], ACT.Relu, bias=b1).then_inc(act_done[s], 1)
                    ac.wait_ge(pool_done[s], after(pool_steps, turn, "x0_lo", NB - 1))
                    for a in range(NB):
                        copy(X[s][:, a, :, :], X[s][:, a, :, :], scale=3.0).then_inc(act_done[s], 1)
                for s in range(STREAMS):
                    for i in range(8):
                        a, pair = i % 4, i // 4
                        from_psum(turn, s, "pair2", i, "z2_hi", ZH[s][:, a, 2 * pair:2 * pair + 2, :], half(s, i, 0))
                for s in range(STREAMS):
                    for b in range(GB):
                        from_psum(turn, s, "t1", b, "t1_hi", TH[s][:, b, :], bias=1.0)
                for l, ks in lots:
                    for s in range(STREAMS):
                        if l:
                            ac.wait_ge(dve_done[s], after(dve_steps, turn, f"euler{ks[0] + 1}", NB - 1))
                        for i in range(NB * GB):
                            a, b = divmod(i, GB)
                            from_psum(turn, s, f"lot{l}", i, f"lot{l}", y_terms(s)[:, :, a, b, :],
                                      bank[s][i % 4][:, 0:LOT * D].rearrange("p (k d) -> p k d", d=D))
                    for k in ks:
                        if k == 0:
                            continue
                        for s in range(STREAMS):
                            if k < EULER_STEPS:
                                ac.wait_ge(pe_done[s], after(pe_steps, turn, f"euler{k}", NB - 1))
                            for a in range(NB):
                                if k < EULER_STEPS:
                                    ac.wait_ge(dve_done[s], after(dve_steps, turn, f"euler{k}", a))
                                else:
                                    ac.wait_ge(act_done[s], after(act_steps, turn, "lot0", a * GB + GB - 1))
                                copy(z2(ZH[s], a), state(s, k, a)).then_inc(act_done[s], 1)
                for s in range(STREAMS):
                    for b in range(GB):
                        from_psum(turn, s, "t2", b, "t2_hi", TH[s][:, b, :], bias=1.0)
                for s in range(STREAMS):
                    for i in range(2 * NB * GB):
                        a, b, j = i // 8, i // 2 % 4, i % 2
                        if a >= 2 and i % 8 == 0:
                            ac.wait_ge(dve_done[s], after(dve_steps, turn, "l2", 4 * (a - 2) + 3))
                        n = (3, 2)[j]
                        from_psum(turn, s, "l2", i, "l2", terms2(s, a)[:, 3 * j:3 * j + n, b, :],
                                  bank[s][i % 4][:, 0:n * D].rearrange("p (k d) -> p k d", d=D))
                for s in range(STREAMS):
                    for a in range(NB):
                        ac.wait_ge(dve_done[s], after(dve_steps, turn, "x2", NB * GB - 1))
                        copy(ZH[s][:, a, :, :], X[s][:, a, :, :]).then_inc(act_done[s], 1)
                for s in range(STREAMS):
                    for b in range(GB):
                        from_psum(turn, s, "gather", b, "gather_hi", TH[s][:, b, :])
                for s in range(STREAMS):
                    for b in range(GB):
                        from_psum(turn, s, "qv", b, "q", l3(s, 0, b), bank[s][b][:, 0:E])
                    for b in range(GB):
                        copy(l3(s, 2, b), bank[s][b][:, E:2 * E]).then_inc(act_done[s], 1)
                for s in range(STREAMS):
                    ac.wait_ge(dve_done[s], after(dve_steps, turn, "seg", 2))
                    A.activation(seg(s, 3), seg(s, 2), ACT.Exp).then_inc(act_done[s], 1)
                for s in range(STREAMS):
                    for b in range(GB):
                        from_psum(turn, s, "wout", b, "wout_hi", ZH[s][:, 0:EB, b, :],
                                  bank[s][b][:, 0:EB * D].rearrange("p (k d) -> p k d", d=D))

        @block.vector
        def _(dv):
            v = nc.vector
            n = 0

            def link(ins):
                nonlocal n
                n += 1
                ins.then_inc(dve_chain, 1)
                dv.wait_ge(dve_chain, n)

            def split(hi, lo, whole):
                link(v.tensor_copy(hi, whole))
                link(v.tensor_tensor(lo, whole, raw(hi), ALU.subtract))

            dv.wait_ge(loaded["adj"], 16)
            link(v.tensor_reduce(r, adj_sb, AX, ALU.max))
            link(v.tensor_reduce(tmp_b, adj_sb, AX, ALU.min))
            link(v.scalar_tensor_tensor(r, tmp_b, -1.0, r, ALU.mult, ALU.max))
            link(v.tensor_scalar(r, r, 1e-30, None, ALU.max))
            link(v.reciprocal(r_inv, r))
            link(v.tensor_scalar(neg_r, r, -1.0, None, ALU.mult))
            link(v.tensor_reduce(row_sum, adj_sb, AX, ALU.add))
            for a in range(NB):
                link(v.tensor_scalar(b_hi[:, a, :], adj_sb[:, a, :], r_inv[:, a:a + 1], None, ALU.mult))
                link(v.scalar_tensor_tensor(rest, raw(b_hi[:, a, :]), neg_r[:, a:a + 1], adj_sb[:, a, :],
                                            ALU.mult, ALU.add))
                link(v.tensor_scalar(b_lo[:, a, :], rest, r_inv[:, a:a + 1], None, ALU.mult))
            link(v.tensor_reduce(tmp_b[:, 0:1], raw(b_lo), AXES, ALU.max))
            link(v.tensor_reduce(tmp_b[:, 1:2], raw(b_lo), AXES, ALU.min))
            v.scalar_tensor_tensor(low_col, tmp_b[:, 1:2], -1.0, tmp_b[:, 0:1], ALU.mult,
                                   ALU.max).then_inc(w_dve_done, 1)
            dv.wait_ge(w_pool_done, after(w_pool_steps, 0, "const"))
            r_diag = picked[:, :, :].rearrange("p a e -> p (a e)")[:, 0:N]
            for a in range(NB):
                link(v.tensor_scalar(r_diag[:, a * P:(a + 1) * P], ident[:, :], r[:, a:a + 1], None, ALU.mult))
            v.memset(tmp_c, 0.0).then_inc(w_dve_done, 1)
            dv.wait_ge(w_pe_done, after(w_pe_steps, 0, "r_row"))
            link(v.tensor_scalar(inexact[:, :], psB[1][0:1, 0:1], 0.0, None, ALU.is_gt))
            v.tensor_copy(r_row[:, :], psB[0][:, :]).then_inc(w_dve_done, 1)

            dv.wait_ge(loaded["w"], 16 * len(loads["w"]))
            dv.wait_ge(w_act_done, after(w_act_steps, 0, "sigmoid"))
            link(v.tensor_scalar(tmp_a, tmp_a, 1.0, None, ALU.add))
            link(v.reciprocal(tmp_a, tmp_a))
            link(v.tensor_scalar(c_neg, tmp_a, -0.5 * DT, None, ALU.mult))
            link(v.scalar_tensor_tensor(c_r, c_neg, -1.0, r, ALU.mult, ALU.mult))
            link(v.tensor_scalar(d_col, d_col, 0.0, 1.0, ALU.max, ALU.min))
            dv.wait_ge(w_act_done, after(w_act_steps, 0, "w_t"))
            v.tensor_scalar(w_t[:, 1, :], w_t[:, 0, :], d_col, None, ALU.mult).then_inc(w_dve_done, 1)
            link(v.tensor_scalar(ident_v, ident[:, :], 1.0 - DT, None, ALU.mult))
            dv.wait_ge(w_pe_done, after(w_pe_steps, 0, "w_eff"))
            v.scalar_tensor_tensor(V, psB[1][:, 0:D], DT, ident_v, ALU.mult, ALU.add).then_inc(w_dve_done, 1)
            mean_col, shift_col = tmp_c[:, 0:1], tmp_c[:, 1:2]
            link(v.tensor_reduce(mean_col, w_in[:, FC, :], AX, ALU.add))
            link(v.tensor_tensor(shift_col, fcb_col, mean_col, ALU.subtract))
            link(v.tensor_scalar(shift_col, shift_col, 1.0 / D, None, ALU.mult))
            link(v.tensor_scalar(chain[:, 0, 0:D], w_in[:, FC, :], shift_col, None, ALU.add))
            v.tensor_scalar(chain[:, 0, D:2 * D], ident[:, :], -1.0 / D, None, ALU.add).then_inc(w_dve_done, 1)
            dv.wait_ge(w_pe_done, after(w_pe_steps, 0, "nv1_t"))
            v.tensor_copy(nv1_t, psA[1][0:RANK, :]).then_inc(w_dve_done, 1)

            dv.wait_ge(loaded["ends"], 16 * len(loads["ends"]))
            link(v.tensor_copy(ends_col, ends_col_i))
            link(v.tensor_copy(ends_row, ends_row_i))
            link(v.scalar_tensor_tensor(key_row, ends_row[:, 0:E], float(E), node_row[:, 0:E], ALU.mult, ALU.add))
            link(v.scalar_tensor_tensor(key_col, ends_col[:, 0:EB], float(E), node_col[:, 0:EB], ALU.mult, ALU.add))
            for e in range(EB):
                link(v.tensor_scalar(less, key_row, key_col[:, e:e + 1], None, ALU.is_lt, ALU.add,
                                     accum_out=rank[:, e:e + 1]))
                link(v.tensor_scalar(perm[:, e, :], node_row[:, 0:E], rank[:, e:e + 1], None, ALU.is_equal))
                for side in range(2):
                    link(v.tensor_scalar(perm_ends[:, e, side * E:(side + 1) * E], perm[:, e, :],
                                         ends_col[:, side * EB + e:side * EB + e + 1], None, ALU.mult))
            v.memset(tmp_c, 0.0).then_inc(w_dve_done, 1)
            dv.wait_ge(w_pe_done, after(w_pe_steps, 0, "ends_row"))
            v.tensor_copy(ends_row, psA[2][:, :]).then_inc(w_dve_done, 1)
            dv.wait_ge(w_dve_done, after(w_dve_steps, 0, "ends_row"))
            dv.wait_ge(w_pe_done, after(w_pe_steps, 0, "src_col"))
            link(v.tensor_copy(src_col, psA[3][:, 0:EB]))
            for a in range(NB):
                link(v.tensor_scalar(one_src[:, a, :], ends_row[:, 0:E], node_col[:, a:a + 1], None, ALU.is_equal))
                link(v.tensor_scalar(E1[:, a, E:2 * E], ends_row[:, E:2 * E], node_col[:, a:a + 1], None,
                                     ALU.is_equal))
                link(v.tensor_tensor(E1[:, a, 0:E], one_src[:, a, :], raw(E1[:, a, E:2 * E]), ALU.add))
            for e in range(EB):
                link(v.tensor_scalar(S1[:, e, :], node_row, src_col[:, e:e + 1], None, ALU.is_equal))
            link(v.memset(edge[:, 0, :], 1.0))
            link(v.tensor_tensor(edge[:, 0, 1:E], ends_row[0:HR, 1:E], ends_row[0:HR, 0:E - 1], ALU.not_equal))
            link(v.tensor_scalar(edge[:, 1, :], edge[:, 0, :], -BIG, None, ALU.mult))
            link(v.tensor_scalar(edge[:, 2, :], edge[:, 0, :], -1.0, 1.0, ALU.mult, ALU.add))
            v.memset(tmp_c, 0.0).then_inc(w_dve_done, 1)

            link(v.tensor_tensor(w_sum[:, 0, :], w_l2[:, 0, :], ident[:, :], ALU.add))
            link(v.tensor_tensor(w_sum[:, 1, :], w_l2[:, 1, :], w_l2[:, 3, :], ALU.add))
            link(v.tensor_tensor(w_sum[:, 2, :], w_l2[:, 2, :], w_l2[:, 4, :], ALU.add))
            link(v.tensor_copy(w_sum[:, 3:5, :], w_l2[:, 5:7, :]))
            v.memset(tmp_c, 0.0).then_inc(w_dve_done, 1)

            for p in range(1, NQ):
                dv.wait_ge(w_pe_done, after(w_pe_steps, 0, "power", p - 1))
                ps = psB[2 + p % 2]
                if p < EULER_STEPS:
                    v.tensor_copy(chain[:, p, :], ps[:, 0:2 * D]).then_inc(w_dve_done, 1)
                else:
                    v.tensor_copy(last_power, ps[:, 0:D]).then_inc(w_dve_done, 1)

            dv.wait_ge(w_pe_done, after(w_pe_steps, 0, "l2_mean", 1))
            link(v.scalar_tensor_tensor(w_sum[:, 0:4, :], psB[0][:, :].rearrange("p (j d) -> p j d", d=D), -1.0 / D,
                                        w_sum[:, 0:4, :], ALU.mult, ALU.add))
            v.scalar_tensor_tensor(w_sum[:, 4, :], psB[1][:, 0:D], -1.0 / D, w_sum[:, 4, :],
                                                ALU.mult, ALU.add).then_inc(w_dve_done, 1)
            dv.wait_ge(w_dve_done, after(w_dve_steps, 0, "l2_w"))
            link(v.scalar_tensor_tensor(w_sum[:, 0, :], b_l2, 1.0 / D, w_sum[:, 0, :], ALU.mult, ALU.add))
            split(VH[:, :, :], VL[:, :, :], w_sum)
            split(w1H[:, :, :], w1L[:, :, :], w_in[:, W1N:W1L + 1, :])
            w2_in = w_in[:, W2N:W2L + 1, :].rearrange("p a d -> p (a d)")
            split(w2H[:, :], w2L[:, :], w2_in)
            dv.wait_ge(w_pe_done, after(w_pe_steps, 0, "g_t"))
            link(v.tensor_copy(w_t, psA[1][:, 0:2 * D].rearrange("p (a d) -> p a d", d=D)))
            split(gH[:, :, :], gL[:, :, :], w_t)
            link(v.tensor_copy(w_out[:, :], psA[1][:, 2 * D:3 * D]))
            for h in range(HEADS):
                at_h = HR - HEADS + h
                link(v.tensor_copy(a_pad[h * DH:(h + 1) * DH, at_h:at_h + 1], a_col[h * DH:(h + 1) * DH, :]))
            v.memset(tmp_c, 0.0).then_inc(w_dve_done, 1)

            for a in range(NB):
                dv.wait_ge(w_pe_done, after(w_pe_steps, 0, "adj_rows", a))
                v.tensor_tensor(picked[:, a, :], psA[2 + a % 2][:, 0:E], raw(E1[:, a, E:2 * E]),
                                             ALU.mult).then_inc(w_dve_done, 1)
            dv.wait_ge(w_pe_done, after(w_pe_steps, 0, "picked"))
            v.tensor_scalar(log_a[:, :], psB[1][0:1, 0:E], 1e-8, None, ALU.add).then_inc(w_dve_done, 1)

            for a in range(NB):
                dv.wait_ge(w_pe_done, after(w_pe_steps, 0, "logits", a))
                link(v.tensor_scalar(soft, psB[2 + a % 2][:, :], 0.0, None, ALU.max, ALU.max,
                                     accum_out=tmp_a[:, a:a + 1]))
                v.tensor_scalar(tmp_b[:, a:a + 1], tmp_a[:, a:a + 1], -1.0, None, ALU.mult).then_inc(w_dve_done, 1)
                dv.wait_ge(w_act_done, after(w_act_steps, 0, "soft", a))
                link(v.reciprocal(tmp_a[:, a:a + 1], tmp_c[:, a:a + 1]))
                v.tensor_scalar(soft, soft, tmp_a[:, a:a + 1], None, ALU.mult, ALU.add,
                                             accum_out=t_sum[:, a:a + 1]).then_inc(w_dve_done, 1)
                dv.wait_ge(w_dve_done, after(w_dve_steps, 0, "t_sum", a))

            for k in range(EULER_STEPS, -1, -1):
                q = q_t[:, EULER_STEPS - k, :]
                p = EULER_STEPS - k
                f_power = last_power if p == EULER_STEPS else chain[:, p, 0:D]
                link(v.tensor_scalar(q, f_power, float(comb(EULER_STEPS, k)), None, ALU.mult))
                for j in range(k, EULER_STEPS):
                    extra = 1.0 if k == 0 and j == 0 else 0.0
                    link(v.scalar_tensor_tensor(q, chain[:, j - k, D:2 * D], DT * comb(j, k) + extra, q,
                                                ALU.mult, ALU.add))
            v.memset(tmp_c, 0.0).then_inc(w_dve_done, 1)
            for i in range(LOTS):
                dv.wait_ge(w_act_done, after(w_act_steps, 0, "q_t", i))
                part = slice(i * LOT, (i + 1) * LOT)
                link(v.tensor_tensor(QL[:, part, :], q_bank[i][:, 0:LOT * D].rearrange("p (k d) -> p k d", d=D),
                                     raw(QH[:, part, :]), ALU.subtract))
            v.memset(tmp_c, 0.0).then_inc(w_dve_done, 1)
            dv.wait_ge(w_dve_done, after(w_dve_steps, 0, "done"))

            with dv.Fori(0, TURNS) as turn:
                def low(s, stage, hi_step, i, lo, hi, part, what, shift=None):
                    dv.wait_ge(pe_done[s], after(pe_steps, turn, stage, i))
                    dv.wait_ge(act_done[s], after(act_steps, turn, hi_step, i))
                    ins = (v.tensor_tensor(lo, part, raw(hi), ALU.subtract) if shift is None else
                           v.scalar_tensor_tensor(lo, part, shift, raw(hi), ALU.add, ALU.subtract))
                    ins.then_inc(dve_done[s], 1)

                def normalize(s, n, src, eps):
                    st, sm = stats[s], small[s]
                    for i in range(NB * GB):
                        v.bn_stats(st[:, i, :], src[s][:, i // GB, i % GB, :]).then_inc(dve_done[s], 1)
                    dv.wait_ge(dve_done[s], after(dve_steps, turn, f"stats{n}", NB * GB - 1))
                    v.tensor_tensor(sm[:, 0, :], st[:, :, 1], st[:, :, 4], ALU.add).then_inc(dve_done[s], 1)
                    v.tensor_tensor(sm[:, 1, :], st[:, :, 1], st[:, :, 4], ALU.subtract).then_inc(dve_done[s], 1)
                    v.tensor_tensor(sm[:, 2, :], st[:, :, 2], st[:, :, 5], ALU.add).then_inc(dve_done[s], 1)
                    dv.wait_ge(dve_done[s], after(dve_steps, turn, f"half_difference{n}"))
                    v.tensor_tensor(sm[:, 3, :], sm[:, 1, :], sm[:, 1, :], ALU.mult).then_inc(dve_done[s], 1)
                    dv.wait_ge(dve_done[s], after(dve_steps, turn, f"square{n}"))
                    v.scalar_tensor_tensor(sm[:, 4, :], sm[:, 3, :], D / 4.0, sm[:, 2, :], ALU.mult, ALU.add).then_inc(dve_done[s], 1)
                    dv.wait_ge(dve_done[s], after(dve_steps, turn, f"spread{n}"))
                    v.tensor_scalar(sm[:, 5, :], sm[:, 4, :], 1.0 / D, eps, ALU.mult, ALU.add).then_inc(dve_done[s], 1)
                    v.tensor_scalar(sm[:, 7, :], sm[:, 0, :], 0.5, None, ALU.mult).then_inc(dve_done[s], 1)
                    dv.wait_ge(dve_done[s], after(dve_steps, turn, f"mean{n}"))
                    dv.wait_ge(pool_done[s], after(pool_steps, turn, f"rstd{n}"))
                    for i in range(NB * GB):
                        b, a = divmod(i, NB)
                        at_i = a * GB + b
                        v.tensor_scalar(X[s][:, a, b, :], src[s][:, a, b, :], sm[:, 7, at_i:at_i + 1],
                                                      sm[:, 6, at_i:at_i + 1], ALU.subtract, ALU.mult).then_inc(dve_done[s], 1)

                for s in range(STREAMS):
                    for b in range(GB):
                        low(s, "t0", "t0_hi", b, TL[s][:, b, :], TH[s][:, b, :], bank[s][b][:, :], "t0_lo")
                for s in range(STREAMS):
                    for b in range(GB):
                        dv.wait_ge(pe_done[s], after(pe_steps, turn, "neigh1", b))
                        v.tensor_tensor(Y[s][:, b * N:(b + 1) * N], bank[s][b][:, :], r_row[:, :],
                                                      ALU.mult).then_inc(dve_done[s], 1)
                for s in range(STREAMS):
                    for i in range(8):
                        a, pair = i % 4, i // 4
                        two = slice(2 * pair, 2 * pair + 2)
                        low(s, "pair2", "z2_hi", i, ZL[s][:, a, two, :], ZH[s][:, a, two, :], half(s, i, 0), "z2_lo")
                        v.tensor_tensor(F[s][:, a, two, :], half(s, i, 1), b2_row[:, :, :], ALU.add).then_inc(dve_done[s], 1)
                for s in range(STREAMS):
                    dv.wait_ge(dve_done[s], after(dve_steps, turn, "loop2", 7))
                    for a in range(NB):
                        dv.wait_ge(pe_done[s], after(pe_steps, turn, "neigh2", a))
                        v.scalar_tensor_tensor(F[s][:, a, :, :], wide(s, a), r[:, a:a + 1],
                                                             F[s][:, a, :, :], ALU.mult, ALU.add).then_inc(dve_done[s], 1)
                    for a in range(NB):
                        dv.wait_ge(dve_done[s], after(dve_steps, turn, "conv2", a))
                        dv.wait_ge(act_done[s], after(act_steps, turn, "x_3", a))
                        v.scalar_tensor_tensor(X[s][:, a, :, :], F[s][:, a, :, :], 0.0, X[s][:, a, :, :],
                                                             ALU.max, ALU.add).then_inc(dve_done[s], 1)
                    dv.wait_ge(dve_done[s], after(dve_steps, turn, "y0", NB - 1))
                    normalize(s, 0, X, 4e-5)
                for s in range(STREAMS):
                    for b in range(GB):
                        low(s, "t1", "t1_hi", b, TL[s][:, b, :], TH[s][:, b, :], bank[s][b][:, :], "t1_lo", 1.0)
                for l, ks in lots:
                    for i_k, k in enumerate(ks):
                        if k == EULER_STEPS:
                            continue
                        for s in range(STREAMS):
                            if k < EULER_STEPS - 1:
                                dv.wait_ge(dve_done[s], after(dve_steps, turn, f"euler{k + 1}", NB - 1))
                            for a in range(NB):
                                dv.wait_ge(act_done[s], after(act_steps, turn, f"lot{l}", a * GB + GB - 1))
                                term = y_terms(s)[:, i_k, a, :, :]
                                v.scalar_tensor_tensor(term, state(s, k + 1, a), c_neg[:, a:a + 1],
                                                                     term, ALU.mult, ALU.add).then_inc(dve_done[s], 1)
                            for a in range(NB):
                                dv.wait_ge(dve_done[s], after(dve_steps, turn, f"local{k}", a))
                                dv.wait_ge(pe_done[s], after(pe_steps, turn, f"euler{k}", a))
                                term = y_terms(s)[:, i_k, a, :, :]
                                v.scalar_tensor_tensor(F[s][:, a, :, :], wide(s, a), c_r[:, a:a + 1],
                                                                     term, ALU.mult, ALU.add).then_inc(dve_done[s], 1)
                for s in range(STREAMS):
                    dv.wait_ge(dve_done[s], after(dve_steps, turn, "euler0", NB - 1))
                    normalize(s, 1, F, 1e-5)
                for s in range(STREAMS):
                    for b in range(GB):
                        low(s, "t2", "t2_hi", b, TL[s][:, b, :], TH[s][:, b, :], bank[s][b][:, :], "t2_lo", 1.0)
                for s in range(STREAMS):
                    for a in range(NB):
                        dv.wait_ge(act_done[s], after(act_steps, turn, "l2", 8 * a + 7))
                        A = [terms2(s, a)[:, j, :, :] for j in range(5)]
                        s_a, t_a = row_sum[:, a:a + 1], t_sum[:, a:a + 1]
                        stt = v.scalar_tensor_tensor
                        stt(A[1], A[2], s_a, A[1], ALU.mult, ALU.add).then_inc(dve_done[s], 1)
                        stt(A[3], A[4], t_a, A[3], ALU.mult, ALU.add).then_inc(dve_done[s], 1)
                        dv.wait_ge(dve_done[s], after(dve_steps, turn, "l2", 4 * a))
                        stt(A[0], A[1], s_a, A[0], ALU.mult, ALU.add).then_inc(dve_done[s], 1)
                        dv.wait_ge(dve_done[s], after(dve_steps, turn, "l2", 4 * a + 2))
                        stt(F[s][:, a, :, :], A[3], t_a, A[0], ALU.mult, ALU.add).then_inc(dve_done[s], 1)
                    dv.wait_ge(dve_done[s], after(dve_steps, turn, "l2", 4 * NB - 1))
                    normalize(s, 2, F, 1e-5)
                for s in range(STREAMS):
                    for b in range(GB):
                        low(s, "gather", "gather_hi", b, TL[s][:, b, :], TH[s][:, b, :], bank[s][b][:, :],
                            "gather_lo")
                for s in range(STREAMS):
                    for b in range(GB):
                        dv.wait_ge(act_done[s], after(act_steps, turn, "q", b))
                        v.scalar_tensor_tensor(l3(s, 1, b), l3(s, 0, b), 0.2, l3(s, 0, b), ALU.mult,
                                                             ALU.max).then_inc(dve_done[s], 1)
                for s in range(STREAMS):
                    first, last = slice(0, E), slice(1, E + 1)
                    back = slice(None, None, -1)
                    score = bank[s][0][0:HR, 0:E]
                    dv.wait_ge(pe_done[s], after(pe_steps, turn, "score"))
                    v.tensor_tensor_scan(seg(s, 0), edge[:, 1, first], score, 0.0, ALU.add, ALU.max).then_inc(dve_done[s], 1)
                    dv.wait_ge(dve_done[s], after(dve_steps, turn, "seg", 0))
                    v.tensor_tensor_scan(seg(s, 1)[:, back], edge[:, 1, last][:, back], seg(s, 0)[:, back],
                                              0.0, ALU.add, ALU.max).then_inc(dve_done[s], 1)
                    dv.wait_ge(dve_done[s], after(dve_steps, turn, "seg", 1))
                    v.tensor_tensor(seg(s, 2), score, seg(s, 1), ALU.subtract).then_inc(dve_done[s], 1)
                    dv.wait_ge(act_done[s], after(act_steps, turn, "exp"))
                    v.tensor_tensor_scan(seg(s, 4), edge[:, 2, first], seg(s, 3), 0.0, ALU.mult, ALU.add).then_inc(dve_done[s], 1)
                    dv.wait_ge(dve_done[s], after(dve_steps, turn, "seg", 3))
                    v.tensor_tensor_scan(seg(s, 5)[:, back], edge[:, 2, last][:, back], seg(s, 4)[:, back],
                                              0.0, ALU.mult, ALU.max).then_inc(dve_done[s], 1)
                    dv.wait_ge(dve_done[s], after(dve_steps, turn, "seg", 4))
                    v.reciprocal(seg(s, 6), seg(s, 5)).then_inc(dve_done[s], 1)
                    dv.wait_ge(dve_done[s], after(dve_steps, turn, "seg", 5))
                    v.tensor_tensor(seg(s, 7), seg(s, 3), seg(s, 6), ALU.mult).then_inc(dve_done[s], 1)
                for s in range(STREAMS):
                    for b in range(GB):
                        dv.wait_ge(pe_done[s], after(pe_steps, turn, "spread", b))
                        dv.wait_ge(act_done[s], after(act_steps, turn, "v", b))
                        v.tensor_tensor(l3(s, 3, b), bank[s][b][:, 0:E], l3(s, 2, b), ALU.mult).then_inc(dve_done[s], 1)
                for s in range(STREAMS):
                    for b in range(GB):
                        low(s, "wout", "wout_hi", b, ZL[s][:, 0:EB, b, :], ZH[s][:, 0:EB, b, :],
                            bank[s][b][:, 0:EB * D].rearrange("p (k d) -> p k d", d=D), "wout_lo")
                for s in range(STREAMS):
                    for a in range(NB):
                        dv.wait_ge(pe_done[s], after(pe_steps, turn, "scatter", a))
                        v.tensor_tensor(F[s][:, a, :, :], wide(s, a), X[s][:, a, :, :], ALU.add).then_inc(dve_done[s], 1)
                    dv.wait_ge(dve_done[s], after(dve_steps, turn, "y3", NB - 1))
                    normalize(s, 3, F, 1e-5)

        @block.tensor
        def _(pt):
            T = nc.tensor

            def products(out_, terms):
                for n, (lhs_t, rhs) in enumerate(terms):
                    last = T.matmul(out_, lhs_t, rhs, start=n == 0, stop=n == len(terms) - 1)
                return last

            def three(lh, ll, rh, rl):
                return [(lh, rh), (lh, rl), (ll, rh)]

            def block_of(i, width=P):
                return slice(i * width, (i + 1) * width)

            pt.wait_ge(w_pool_done, after(w_pool_steps, 0, "const"))
            pt.wait_ge(w_dve_done, after(w_dve_steps, 0, "b_split"))
            for i in range(2 * NB):
                if i >= 4:
                    pt.wait_ge(w_act_done, after(w_act_steps, 0, "b_t", i - 4))
                for a in range(NB):
                    part = (b_hi if i < NB else b_lo)[:, a, block_of(i % NB)]
                    last = T.transpose(psA[i % 4][:, block_of(a)], raw(part), ident[:, :])
                last.then_inc(w_pe_done, 1)
            pt.wait_ge(w_dve_done, after(w_dve_steps, 0, "r_diag"))
            r_diag = picked[:, :, :].rearrange("p a e -> p (a e)")[:, 0:N]
            products(psB[1][0:1, 0:1], [(ones[:, 0:1], low_col)])
            products(psB[0][:, :], [(ones[:, :], r_diag)]).then_inc(w_pe_done, 1)
            pt.wait_ge(loaded["w"], 16 * len(loads["w"]))
            pt.wait_ge(w_act_done, after(w_act_steps, 0, "b_t", 7))
            T.transpose(psA[0][:, 0:D], w_in[:, WE, :], ident[:, :]).then_inc(w_pe_done, 1)
            pt.wait_ge(w_dve_done, after(w_dve_steps, 0, "w_by_d"))
            products(psB[1][:, 0:D], [(w_t[:, 1, :], w_t[:, 0, :])]).then_inc(w_pe_done, 1)
            for a in range(NB):
                last = T.transpose(psA[1][0:RANK, block_of(a)], nv1[:, a, :], ident[:, :])
            last.then_inc(w_pe_done, 1)
            pt.wait_ge(w_dve_done, after(w_dve_steps, 0, "perm"))
            products(psA[2][:, :], [(ones[:, :], perm_ends[:, e, :]) for e in range(EB)]).then_inc(w_pe_done, 1)
            for e in range(EB):
                last = products(psA[3][:, e:e + 1], [(perm[:, f, block_of(e)], ends_col[:, f:f + 1])
                                                     for f in range(EB)])
            last.then_inc(w_pe_done, 1)
            for p in range(1, NQ):
                if p == 1:
                    pt.wait_ge(w_dve_done, after(w_dve_steps, 0, "chain0"))
                else:
                    pt.wait_ge(w_dve_done, after(w_dve_steps, 0, "power", p - 2))
                n = 2 * D if p < EULER_STEPS else D
                products(psB[2 + p % 2][:, 0:n], [(V, chain[:, p - 1, 0:n])]).then_inc(w_pe_done, 1)
            products(psB[0][:, :], [(ones[:, :], w_sum[:, 0:4, :])]).then_inc(w_pe_done, 1)
            products(psB[1][:, 0:D], [(ones[:, :], w_sum[:, 4, :])]).then_inc(w_pe_done, 1)
            for i, w in enumerate((WLIN, WVAL, WOUT)):
                last = T.transpose(psA[1][:, block_of(i)], w_in[:, w, :], ident[:, :])
            last.then_inc(w_pe_done, 1)
            for m in range(NB):
                if m >= 2:
                    pt.wait_ge(w_dve_done, after(w_dve_steps, 0, "picked", m - 2))
                products(psA[2 + m % 2][:, 0:E], [(adj_sb[:, a, block_of(m)], one_src[:, a, :])
                                                              for a in range(NB)]).then_inc(w_pe_done, 1)
            pt.wait_ge(w_dve_done, after(w_dve_steps, 0, "picked", NB - 1))
            products(psB[1][0:1, 0:E], [(ones[:, 0:1], picked[:, m, :]) for m in range(NB)]).then_inc(w_pe_done, 1)
            for a in range(NB):
                pt.wait_ge(w_dve_done, after(w_dve_steps, 0, "log_in" if a < 2 else "rowmax", a - 2 if a >= 2 else 0))
                products(psB[2 + a % 2][:, :], [(nv1_t[:, block_of(a)], nv2)]).then_inc(w_pe_done, 1)
            pt.wait_ge(w_dve_done, after(w_dve_steps, 0, "q"))
            for i in range(LOTS):
                for k in range(LOT):
                    last = T.transpose(q_bank[i][:, block_of(k)], q_t[:, i * LOT + k, :], ident[:, :])
                last.then_inc(w_pe_done, 1)
            pt.wait_ge(w_dve_done, after(w_dve_steps, 0, "done"))
            has_low = pt.value_load(inexact[0:1, 0:1])

            with pt.Fori(0, TURNS) as turn:
                def begin(s, stage, i, *needs):
                    if bank_user[stage, i] is not None:
                        old, j = bank_user[stage, i]
                        done, steps, what = last_reader[old]
                        needs += ((done, steps, what, 2 if old == "score" else j),)
                    for done, steps in ((act_done, act_steps), (dve_done, dve_steps), (pool_done, pool_steps)):
                        values = [after(steps, 0, what, j) for d, _, what, j in needs if d is done]
                        if values:
                            pt.wait_ge(done[s], turn * len(steps) + max(values))

                def chunk(s, stage, i, terms, out_=None, needs=()):
                    begin(s, stage, i, *needs)
                    products(bank[s][i % 4][:, :] if out_ is None else out_, terms).then_inc(pe_done[s], 1)

                def transposes(s, stage, b, *needs):
                    begin(s, stage, b, *needs)
                    for a in range(NB):
                        last = T.transpose(bank[s][b][:, block_of(a)], X[s][:, a, b, :], ident[:, :])
                    last.then_inc(pe_done[s], 1)

                def by_b(s, stage, hi_step, lo_step, n, operands):
                    done, steps, lo_what = lo_step
                    for a in range(4):
                        i = 0 if n == NB else n - 1
                        begin(s, stage, a, (act_done, act_steps, hi_step, i), lo_step + (i,))
                        T.matmul(bank[s][a][:, :], *operands(a, 0, BTH, ZH), start=True, stop=False)
                    with pt.If(has_low != 0):
                        pt.wait_ge(act_done[s], after(act_steps, turn, hi_step, n - 1))
                        for a in range(4):
                            for m in range(NB):
                                T.matmul(bank[s][a][:, :], *operands(a, m, BTL, ZH), start=False, stop=False)
                    for a in range(4):
                        for m in range(NB):
                            if n == NB and a == 0 and m > 0:
                                pt.wait_ge(act_done[s], after(act_steps, turn, hi_step, m))
                                pt.wait_ge(done[s], after(steps, turn, lo_what, m))
                            if m > 0:
                                T.matmul(bank[s][a][:, :], *operands(a, m, BTH, ZH), start=False, stop=False)
                            last = T.matmul(bank[s][a][:, :], *operands(a, m, BTH, ZL), start=False,
                                            stop=m == NB - 1)
                        last.then_inc(pe_done[s], 1)

                def left(s):
                    return lambda a, m, b_t, z: (b_t[:, m, block_of(a)], z[s][:, m, :, :])

                def right(s):
                    return lambda a, m, b_t, z: (z[s][:, m, a, :], b_t[:, m, :])

                for s in range(STREAMS):
                    pt.wait_ge(x_loaded[s], (turn + 1) * (16 * NB))
                    for b in range(GB):
                        transposes(s, "t0", b)
                for s in range(STREAMS):
                    by_b(s, "neigh1", "x0_hi", (pool_done, pool_steps, "x0_lo"), NB, right(s))
                for s in range(STREAMS):
                    for b in range(GB):
                        chunk(s, "conv1", b,
                              three(w1H[:, 0, :], w1L[:, 0, :], ZH[s][:, :, b, :], ZL[s][:, :, b, :])
                              + three(w1H[:, 1, :], w1L[:, 1, :], TH[s][:, b, :], TL[s][:, b, :]),
                              needs=((act_done, act_steps, "neigh1_hi", b), (pool_done, pool_steps, "neigh1_lo", b), (act_done, act_steps, "t0_hi", b),
                                     (dve_done, dve_steps, "t0_lo", b)))
                for s in range(STREAMS):
                    for i in range(8):
                        a, pair = i % 4, i // 4
                        begin(s, "pair2", i, (act_done, act_steps, "h1_hi", 2 * pair + 1), (pool_done, pool_steps, "h1_lo", 2 * pair + 1))
                        for c in range(2):
                            b = 2 * pair + c
                            last = products(bank[s][i % 4][:, block_of(c, 2 * D)],
                                            three(TH[s][:, b, block_of(a)], TL[s][:, b, block_of(a)],
                                                  w2H[:, :], w2L[:, :]))
                        last.then_inc(pe_done[s], 1)
                for s in range(STREAMS):
                    by_b(s, "neigh2", "z2_hi", (dve_done, dve_steps, "z2_lo"), 8, left(s))
                for s in range(STREAMS):
                    for b in range(GB):
                        transposes(s, "t1", b, (dve_done, dve_steps, "x0", b * NB + NB - 1))
                for l, ks in lots:
                    for s in range(STREAMS):
                        for i in range(NB * GB):
                            a, b = divmod(i, GB)
                            part = slice(l * LOT, (l + 1) * LOT)
                            chunk(s, f"lot{l}", i, three(TH[s][:, b, block_of(a)], TL[s][:, b, block_of(a)],
                                                         QH[:, part, :], QL[:, part, :]),
                                  bank[s][i % 4][:, 0:LOT * D],
                                  ((act_done, act_steps, "t1_hi", b), (dve_done, dve_steps, "t1_lo", b)))
                    for k in ks:
                        if k < EULER_STEPS:
                            for s in range(STREAMS):
                                by_b(s, f"euler{k}", f"euler{k + 1}_hi",
                                     (pool_done, pool_steps, f"euler{k + 1}_lo"), NB, left(s))
                for s in range(STREAMS):
                    for b in range(GB):
                        transposes(s, "t2", b, (dve_done, dve_steps, "x1", b * NB + NB - 1))
                for s in range(STREAMS):
                    for i in range(2 * NB * GB):
                        a, b, j = i // 8, i // 2 % 4, i % 2
                        part = (slice(0, 3), slice(3, 5))[j]
                        chunk(s, "l2", i, three(TH[s][:, b, block_of(a)], TL[s][:, b, block_of(a)],
                                                VH[:, part, :], VL[:, part, :]),
                              bank[s][i % 4][:, 0:(3, 2)[j] * D], ((act_done, act_steps, "t2_hi", b), (dve_done, dve_steps, "t2_lo", b)))
                for s in range(STREAMS):
                    pt.wait_ge(act_done[s], after(act_steps, turn, "x3_hi", NB - 1))
                    pt.wait_ge(pool_done[s], after(pool_steps, turn, "x3_lo", NB - 1))
                    for b in range(GB):
                        chunk(s, "gather", b, [(z[s][:, m, b, :], E1[:, m, :]) for m in range(NB) for z in (ZH, ZL)])
                for s in range(STREAMS):
                    for b in range(GB):
                        begin(s, "qv", b, (act_done, act_steps, "gather_hi", b), (dve_done, dve_steps, "gather_lo", b))
                        for side in range(2):
                            part = block_of(side, E)
                            last = products(bank[s][b][:, part], three(gH[:, side, :], gL[:, side, :],
                                                                       TH[s][:, b, part], TL[s][:, b, part]))
                        last.then_inc(pe_done[s], 1)
                for s in range(STREAMS):
                    lo = HR - HEADS
                    chunk(s, "score", 0, [(a_pad[:, lo - HEADS * b:lo - HEADS * b + HR], l3(s, 1, b))
                                          for b in range(GB)] + [(ones[0:1, 0:HR], log_a[:, :])],
                          bank[s][0][0:HR, 0:E], ((dve_done, dve_steps, "leaky", GB - 1),))
                for s in range(STREAMS):
                    for b in range(GB):
                        chunk(s, "spread", b, [(head_of[:, b, :], seg(s, 7))], bank[s][b][:, 0:E],
                              ((dve_done, dve_steps, "seg", 6),))
                for s in range(STREAMS):
                    for b in range(GB):
                        begin(s, "wout", b, (dve_done, dve_steps, "mix", b))
                        for e in range(EB):
                            last = products(bank[s][b][:, block_of(e)], [(l3(s, 3, b)[:, block_of(e)], w_out[:, :])])
                        last.then_inc(pe_done[s], 1)
                for s in range(STREAMS):
                    for a in range(NB):
                        chunk(s, "scatter", a, [(S1[:, e, block_of(a)], z[s][:, e, :, :])
                                                for e in range(EB) for z in (ZH, ZL)],
                              needs=((act_done, act_steps, "wout_hi", GB - 1), (dve_done, dve_steps, "wout_lo", GB - 1)))


NAMES = ["x", "adj", "L0_gnn_w1_loop", "L0_gnn_w1_neigh", "L0_gnn_b1", "L0_gnn_w2_loop", "L0_gnn_w2_neigh",
         "L0_gnn_b2", "L1_gnn_alpha_train", "L1_gnn_w", "L1_gnn_d", "L1_gnn_fc_in_w", "L1_gnn_fc_in_b",
         "L2_gnn_node_vec1", "L2_gnn_node_vec2", "L2_gnn_W", "L2_gnn_b", "L3_gnn_W_lin", "L3_gnn_W_val",
         "L3_gnn_a", "L3_gnn_W_out", "L3_gnn_src", "L3_gnn_dst"]


def kernel(**inputs):
    import numpy as np
    import concourse.bacc as bacc
    from concourse.bass_utils import run_bass_kernel_spmd

    nc = bacc.Bacc("TRN2", target_bir_lowering=False, num_devices=1)
    arrays, tensors = {}, {}
    for name in NAMES:
        a = np.ascontiguousarray(inputs[name])
        arrays[f"in_{name}"] = a
        tensors[name] = nc.dram_tensor(f"in_{name}", a.shape, mybir.dt.from_np(a.dtype), kind="ExternalInput").ap()
    out = nc.dram_tensor("out_x", arrays["in_x"].shape, F32, kind="ExternalOutput").ap()
    build_program(nc, tensors, out)
    result = run_bass_kernel_spmd(nc, [arrays], core_ids=[0])
    return result.results[0]["out_x"]
```

```python
from contextlib import ExitStack
from math import comb

import concourse.bass as bass
from concourse import mybir

F32 = mybir.dt.float32
F32R = mybir.dt.float32r
I32 = mybir.dt.int32
ALU = mybir.AluOpType
ACT = mybir.ActivationFunctionType
AX = mybir.AxisListType.X

P = 128
STREAMS = 2
EULER_STEPS = 8
LOT = 3
BIG = 3.0e38


def numbered(order):
    listed = [(what, i) for whats, n in order for i in range(n) for what in whats.split("+")]
    return {step: place + 1 for place, step in enumerate(listed)}


def after(steps, turn, what, i=0):
    return turn * len(steps) + steps[what, i]


def build_program(nc, t, out):
    B, N, D = t["x"].shape
    NB = N // P
    E = t["L3_gnn_src"].shape[0]
    EB = E // P
    HEADS, DH = t["L3_gnn_a"].shape
    RANK = t["L2_gnn_node_vec1"].shape[1]
    GB = 512 // D
    TURNS = B // (GB * STREAMS)
    W = GB * D
    DT = 1.0 / EULER_STEPS
    NQ = EULER_STEPS + 1
    LOTS = NQ // LOT
    HR = GB * HEADS
    assert D == P and W == 512 and NB == 4 and EB == 2 and TURNS * GB * STREAMS == B and NQ % LOT == 0

    ctx = ExitStack()
    with ctx:
        def sb(name, shape, dt=F32):
            return ctx.enter_context(nc.sbuf_tensor(name, shape, dt))

        def sem(name):
            return ctx.enter_context(nc.semaphore(name))

        def raw(ap):
            return ap.bitcast(F32)

        X = [sb(f"X{s}", [P, NB, GB, D]) for s in range(STREAMS)]
        ZH = [sb(f"ZH{s}", [P, NB, GB, D], F32R) for s in range(STREAMS)]
        ZL = [sb(f"ZL{s}", [P, NB, GB, D], F32R) for s in range(STREAMS)]
        TH = [sb(f"TH{s}", [P, GB, N], F32R) for s in range(STREAMS)]
        TL = [sb(f"TL{s}", [P, GB, N], F32R) for s in range(STREAMS)]
        F = [sb(f"F{s}", [P, NB, GB, D]) for s in range(STREAMS)]
        Y = [sb(f"Y{s}", [P, LOT * NB * GB * D]) for s in range(STREAMS)]
        stats = [sb(f"stats{s}", [P, NB * GB, 6]) for s in range(STREAMS)]
        small = [sb(f"small{s}", [P, 8, NB * GB]) for s in range(STREAMS)]

        ident = sb("ident", [P, P])
        ones = sb("ones", [P, P])
        minus_half = sb("minus_half", [P, NB * GB])
        BTH = sb("BTH", [P, NB, N], F32R)
        BTL = sb("BTL", [P, NB, N], F32R)
        r_row = sb("r_row", [P, N])
        w1H = sb("w1H", [P, 2, D], F32R)
        w1L = sb("w1L", [P, 2, D], F32R)
        w2H = sb("w2H", [P, 2 * D], F32R)
        w2L = sb("w2L", [P, 2 * D], F32R)
        b2_row = sb("b2_row", [P, 2, D])
        QH = sb("QH", [P, NQ, D], F32R)
        QL = sb("QL", [P, NQ, D], F32R)
        VH = sb("VH", [P, 5, D], F32R)
        VL = sb("VL", [P, 5, D], F32R)
        gH = sb("gH", [P, 2, D], F32R)
        gL = sb("gL", [P, 2, D], F32R)
        w_out = sb("w_out", [P, D])
        E1 = sb("E1", [P, NB, 2 * E], F32R)
        S1 = sb("S1", [P, EB, N], F32R)
        head_of = sb("head_of", [HR, GB, D])
        a_pad = sb("a_pad", [P, 2 * HR - HEADS])
        edge = sb("edge", [HR, 3, E + 1])
        log_a = sb("log_a", [1, E])
        inexact = sb("inexact", [1, 1], I32)
        cols = sb("cols", [P, 56])
        names = {}

        def col(name, n=1):
            if name not in names:
                names[name] = sum(k for _, k in names.values()), n
            at, k = names[name]
            assert at + k <= 56
            return cols[:, at:at + k]

        r, r_inv, neg_r, row_sum, c_neg, c_r, t_sum, b1 = (
            col(x, n) for x, n in (("r", NB), ("r_inv", NB), ("neg_r", NB), ("row_sum", NB), ("c_neg", NB),
                                   ("c_r", NB), ("t_sum", NB), ("b1", 1)))

        at = {}

        def scratch(where, shape, parts=P):
            whole = regions[where]
            n = 1
            for k in shape:
                n *= k
            lo = at.get(where, 0)
            at[where] = lo + n
            assert at[where] <= whole.shape[1], (where, at)
            v = whole[0:parts, lo:lo + n]
            if len(shape) == 2:
                v = v.rearrange("p (a b) -> p a b", b=shape[1])
            return v

        def flat(tile):
            return tile[:, :, :, :].rearrange("p a b c -> p (a b c)")

        def flat3(tile):
            return tile[:, :, :].rearrange("p a b -> p (a b)")

        regions = {"F1": flat(F[1]), "ZH1": flat(ZH[1]), "ZL1": flat(ZL[1]), "TH1": flat3(TH[1]),
                   "TL1": flat3(TL[1]), "X1": flat(X[1]), "Y0": Y[0][:, 2 * NB * GB * D:], "Y1": Y[1][:, :]}
        adj_sb = scratch("F1", [NB, N])
        b_hi, b_lo = scratch("ZH1", [NB, N]), scratch("ZL1", [NB, N])
        w_in = scratch("Y0", [9, D])
        W1N, W1L, W2N, W2L, WE, FC, WLIN, WVAL, WOUT = range(9)
        w_l2 = scratch("Y0", [7, D])
        node_row = scratch("Y1", [N])
        node_col = scratch("Y1", [NB])
        ends_row_i = scratch("Y1", [2 * E]).bitcast(I32)
        ends_col_i = scratch("Y1", [2 * EB]).bitcast(I32)
        ends_col = scratch("Y1", [2 * EB])
        key_row = scratch("Y1", [E])
        key_col = scratch("Y1", [EB])
        rank = scratch("Y1", [EB])
        rest = scratch("Y1", [N])
        less = scratch("TH1", [E])
        perm = scratch("TH1", [EB, E])
        perm_ends = scratch("TH1", [EB, 2 * E])
        ends_row = scratch("TL1", [2 * E])
        one_src = scratch("TL1", [NB, E])
        src_col = scratch("Y1", [EB])
        picked = scratch("Y1", [NB, E])
        all_picked = picked[:, :, :].rearrange("p a e -> p (a e)")
        r_diag, rest_abs = all_picked[:, 0:N], all_picked[:, N:2 * N]
        soft = all_picked[:, 0:N]
        power_0 = scratch("X1", [3, D])
        power_1 = scratch("X1", [3, D])
        powers = scratch("Y1", [(EULER_STEPS - 2) // 2, 4 * D])
        w_t = scratch("X1", [2, D])
        V4 = scratch("X1", [D])
        nv1 = scratch("X1", [NB, RANK])
        b_l2 = scratch("Y1", [D])
        w_sum = scratch("X1", [5, D])
        ident_v = scratch("Y1", [D])
        last_power = scratch("X1", [D])
        nv1_t = scratch("Y1", [N], RANK)
        nv2 = scratch("Y1", [N], RANK)
        q_parts = {k: [(k, float(comb(EULER_STEPS, k)))]
                   + [(j, DT * comb(j, k) + (1.0 if k == 0 and j == 0 else 0.0)) for j in range(k, EULER_STEPS)]
                   for k in range(NQ)}
        factors = sorted({f for parts in q_parts.values() for _, f in parts} - {1.0})
        blocks = [flat(z)[:, lo:lo + D] for z in (ZH[1], ZL[1]) for lo in range(0, NB * GB * D, D)]
        ident_by = {1.0: ident[:, :], **dict(zip(factors, blocks, strict=False))}
        V, V2 = power_0[:, 0, :], power_1[:, 0, :]

        def power(p, part):
            if p < 2:
                return (power_0, power_1)[p][:, 1 + part, :]
            lo = (p % 2 * 2 + part) * D
            return powers[:, p // 2 - 1, lo:lo + D]

        a_col, d_col, fcb_col, alpha, tmp_a, tmp_b, tmp_c, mean_col, shift_col = (
            col(x, n) for x, n in (("a", 1), ("d", 1), ("fcb", 1), ("alpha", NB), ("tmp_a", NB), ("tmp_b", NB),
                                   ("tmp_c", NB), ("mean", 1), ("shift", 1)))
        low_sum, pool_junk = col("low", NB), col("junk", 1)

        bank = [[ctx.enter_context(nc.psum_tensor(f"bank{s}_{j}", [P, 512], F32)) for j in range(4)]
                for s in range(STREAMS)]

        def norm(n):
            return ([(f"{what}{n}", 1) for what in ("mean2", "half_difference", "m2", "square", "spread",
                                                    "variance", "mean")]
                    + [(f"x{n}", NB * GB // 2)])

        def with_stats(what, n):
            return "+".join([what] + [f"stats{n}_{b}" for b in range(GB)])

        lots = [(l, [EULER_STEPS - l * LOT - i for i in range(LOT)]) for l in range(LOTS)]
        pe_order = [("t0", 4), ("neigh1", 4), ("conv1", 4), ("pair2", 8), ("neigh2", 4), ("t1", 4)]
        act_order = [("x0_hi", 4), ("t0_hi", 4), ("neigh1_hi", 4), ("h1+h1_hi", 4), ("x_3", 4), ("z2_hi", 8),
                     ("x0", NB * GB // 2), ("t1_hi", 4)]
        dve_order = [("t0_lo", 4), ("neigh1", 4), ("z2_lo+loop2", 8), (with_stats("conv2+y0", 0), NB)] \
            + norm(0) + [("t1_lo", 4)]
        pool_order = [("x0_lo", 4), ("neigh1_lo", 4), ("h1_lo", 4), ("rstd0+shift0", 1)]
        for l, ks in lots:
            pe_order.append((f"lot{l}", NB * GB))
            act_order.append((f"lot{l}", NB * GB))
            for k in ks:
                if k < EULER_STEPS:
                    pe_order.append((f"euler{k}", NB))
                    dve_order += [(f"local{k}", NB), (f"euler{k}" if k else with_stats("euler0", 1), NB)]
                if k > 0:
                    act_order.append((f"euler{k}_hi", NB))
                    pool_order.append((f"euler{k}_lo", NB))
        dve_order += norm(1) + [("t2_lo", 4)] + [(with_stats("l2_sum0+l2_sum1+l2_sum2+l2_sum3", 2), NB)] + norm(2)
        pool_order += [("rstd1+shift1", 1), ("rstd2+shift2", 1), ("x3_lo", NB // 2), ("rstd3+shift3", 1)]
        pe_order += [("t2", 4), ("l2", 2 * NB * GB), ("gather", 4), ("qv", 4), ("score", 1), ("spread", 4),
                     ("wout", 4), ("scatter", 4)]
        act_order += [("x1", NB * GB // 2), ("t2_hi", 4), ("l2", 2 * NB * GB), ("x2", NB * GB // 2), ("x3_hi", 4),
                      ("gather_hi", 4), ("q", 4), ("v", 4), ("exp", 1), ("wout_hi", 4), ("x3", NB * GB // 2)]
        dve_order += [("x3_lo", NB // 2), ("gather_lo", 4), ("leaky", 4), ("seg", 7), ("mix", 4),
                      ("wout_lo", 4), (with_stats("y3", 3), NB)] + norm(3)

        pe_steps = numbered(pe_order)
        pe_done = [sem(f"pe_done{s}") for s in range(STREAMS)]
        act_steps = numbered(act_order)
        act_done = [sem(f"act_done{s}") for s in range(STREAMS)]
        dve_steps = numbered(dve_order)
        dve_done = [sem(f"dve_done{s}") for s in range(STREAMS)]
        pool_steps = numbered(pool_order)
        pool_done = [sem(f"pool_done{s}") for s in range(STREAMS)]
        x_loaded = [sem(f"x_loaded{s}") for s in range(STREAMS)]
        y_stored = [sem(f"y_stored{s}") for s in range(STREAMS)]

        last_reader = {stage: (dve_done, dve_steps, what) for stage, what in (
            ("t0", "t0_lo"), ("neigh1", "neigh1"), ("pair2", "loop2"), ("neigh2", "conv2"), ("t1", "t1_lo"),
            ("t2", "t2_lo"), ("gather", "gather_lo"), ("score", "seg"), ("spread", "mix"), ("wout", "wout_lo"),
            ("scatter", "y3"))}
        last_reader.update({stage: (act_done, act_steps, what) for stage, what in (
            ("conv1", "h1_hi"), ("l2", "l2"), ("qv", "v"))})
        for l, ks in lots:
            last_reader[f"lot{l}"] = (act_done, act_steps, f"lot{l}")
            for k in ks:
                last_reader[f"euler{k}"] = (dve_done, dve_steps, f"euler{k}")
        bank_user = {}
        before = {}
        for stage, n in pe_order:
            for i in range(n):
                bank_user[stage, i] = before.get(i % 4)
                before[i % 4] = (stage, i)

        loads = {
            "adj": [(adj_sb, t["adj"].rearrange("(a p) m -> p a m", p=P))],
            "w0": [(w_in[:, W1N, :], t["L0_gnn_w1_neigh"]), (w_in[:, W1L, :], t["L0_gnn_w1_loop"]),
                   (w_in[:, W2N, :], t["L0_gnn_w2_neigh"]), (w_in[:, W2L, :], t["L0_gnn_w2_loop"]),
                   (b1, t["L0_gnn_b1"].rearrange("(p a) -> p a", a=1)),
                   (b2_row[:, 0, :], t["L0_gnn_b2"].partition_broadcast(P)),
                   (b2_row[:, 1, :], t["L0_gnn_b2"].partition_broadcast(P))],
            "w": [(w_in[:, WE, :], t["L1_gnn_w"]), (w_in[:, FC, :], t["L1_gnn_fc_in_w"]),
                  (fcb_col, t["L1_gnn_fc_in_b"].rearrange("(p a) -> p a", a=1)),
                  (d_col, t["L1_gnn_d"].rearrange("(p a) -> p a", a=1)),
                  (alpha, t["L1_gnn_alpha_train"].rearrange("(a p) -> p a", p=P)),
                  (nv1, t["L2_gnn_node_vec1"].rearrange("(a p) k -> p a k", p=P)),
                  (nv2, t["L2_gnn_node_vec2"]),
                  (w_in[:, WLIN, :], t["L3_gnn_W_lin"]), (w_in[:, WVAL, :], t["L3_gnn_W_val"]),
                  (w_in[:, WOUT, :], t["L3_gnn_W_out"]),
                  (a_col, t["L3_gnn_a"].rearrange("h (d a) -> (h d) a", a=1)),
                  (w_l2, t["L2_gnn_W"].rearrange("(a p) n -> p a n", p=P)),
                  (b_l2, t["L2_gnn_b"].partition_broadcast(P))],
            "ends": [(ends_row_i[:, 0:E], t["L3_gnn_src"].partition_broadcast(P)),
                     (ends_row_i[:, E:2 * E], t["L3_gnn_dst"].partition_broadcast(P)),
                     (ends_col_i[:, 0:EB], t["L3_gnn_src"].rearrange("(a p) -> p a", p=P)),
                     (ends_col_i[:, EB:2 * EB], t["L3_gnn_dst"].rearrange("(a p) -> p a", p=P))],
        }
        loaded = {what: sem(f"{what}_loaded") for what in loads}
        w_dve_done = sem("w_dve_done")
        w_dve_steps = numbered([("b_hi", NB), ("r_diag", 1), ("b_lo", NB), ("r_row", 1), ("inexact", 1), ("w_by_d", 1),
                                ("v", 1), ("power0", 1), ("nv1_t", 1), ("perm", 1), ("ends_row", 1), ("src_col", 1),
                                ("power", 5), ("last_power", 1), ("one_hot", 1), ("l2_sum", 1), ("l2_w", 1),
                                ("weights", 1), ("picked", NB), ("log_in", 1), ("rowmax+t_sum", NB),
                                ("done", 1)])
        w_act_done = sem("w_act_done")
        w_act_steps = numbered([("b_t", NB), ("low_sum+b_lo_t", NB), ("sigmoid", 1), ("w_t", 1), ("log", 1),
                                ("soft", NB), ("q_t", LOTS)])
        w_pe_done = sem("w_pe_done")
        w_pe_steps = numbered([("b_t", NB), ("r_row", 1), ("b_lo_t", NB), ("low", 1), ("w_t", 1), ("w_eff", 1),
                               ("nv1_t", 1), ("ends_row", 1), ("src_col", 1), ("power", 6),
                               ("l2_mean", 2), ("g_t", 1), ("adj_rows", NB), ("picked", 1), ("logits", NB),
                               ("q_t", LOTS)])
        w_pool_done = sem("w_pool_done")
        w_pool_steps = numbered([("const", 1), ("one_hot", 1), ("q", 1)])
        w_bank = bank[1]
        pool_chain, dve_chain = sem("pool_chain"), sem("dve_chain")

        prepare = """w.adj w.low w.w0 w.v 0.x0 0.t0 0.neigh1 0.conv1 w.edges w.powers w.one_hot 0.triple 0.pair2
            w.l2_mean w.weights w.picked w.soft 0.neigh2 w.q 0.stats.0 w.end 0.norm.0 0.t1""".split()
        in_turn = """1.x0 0.lot.0.0 1.t0 0.lot.0.1 0.lot.0.2 1.neigh1 0.lot.0.3 0.split.8 0.local.7 1.conv1 1.triple
            0.euler.7 1.pair2 0.local.6 0.euler.6 1.neigh2 0.lot.1.0 0.lot.1.1 0.lot.1.2 0.lot.1.3 1.stats.0
            0.local.5 1.norm.0 0.euler.5 0.local.4 1.t1 0.euler.4 0.local.3 1.lot.0.0 1.lot.0.1 0.euler.3
            0.lot.2.0 1.lot.0.2 0.lot.2.1 0.lot.2.2 0.lot.2.3 0.local.2 1.lot.0.3 1.split.8 0.euler.2 0.local.1
            1.local.7 1.euler.7 1.local.6 0.euler.1 0.local.0 1.euler.6 0.euler.0 1.lot.1.0 1.lot.1.1 0.stats.1
            1.lot.1.2 1.lot.1.3 0.norm.1 1.local.5 1.euler.5 0.t2 1.local.4 0.l2.0 0.l2.1 1.euler.4 1.local.3
            0.l2.2 0.l2.3 1.euler.3 1.lot.2.0 0.stats.2 1.lot.2.1 1.lot.2.2 1.lot.2.3 0.norm.2 1.local.2 0.x3
            1.euler.2 1.local.1 0.gather 0.qv 0.score 1.euler.1 0.spread 1.local.0 0.wout 1.euler.0 1.stats.1
            0.scatter 1.norm.1 1.t2 0.stats.3 1.l2.0 1.l2.1 1.l2.2 1.l2.3 1.stats.2 0.norm.3 +0.x0 +0.t0
            1.norm.2 1.x3 +0.neigh1 1.gather 1.qv 1.score +0.conv1 1.spread +0.triple +0.pair2 1.wout +0.neigh2
            +0.stats.0 1.scatter 1.stats.3 +0.norm.0 +0.t1 1.norm.3""".split()
        last_turn = [stage for stage in in_turn if stage[0] != "+"]

        def run(stages, order, turn):
            for name in order:
                stream, what, *index = name.split(".")
                if what in stages:
                    if stream == "w":
                        stages[what]()
                    else:
                        ahead = 1 if stream[0] == "+" else 0
                        stages[what](turn + ahead, int(stream[-1]), *(int(i) for i in index))

        def wide(s, a):
            return bank[s][a][:, :].rearrange("p (b d) -> p b d", d=D)

        def y4(s, b):
            return Y[s][:, b * N:(b + 1) * N].rearrange("p (a n) -> p a n", a=NB)

        def y4_flat(s, b):
            return Y[s][:, b * N:(b + 1) * N]

        def h1(s, b):
            return Y[s][:, (GB + b) * N:(GB + b + 1) * N]

        def z2(z, a):
            return z[:, a, :, :]

        def y_terms(s):
            return Y[s][:, :].rearrange("p (k a b d) -> p k a b d", k=LOT, a=NB, b=GB)

        def state(s, k, a):
            return y_terms(s)[:, 0, a, :, :] if k == EULER_STEPS else F[s][:, a, :, :]

        def half(s, i, part):
            return bank[s][i % 4][:, :].rearrange("p (b w d) -> p b w d", b=2, w=2)[:, :, part, :]

        def terms2(s, a):
            lo = a % 2 * 5 * W
            return Y[s][:, lo:lo + 5 * W].rearrange("p (j b d) -> p j b d", j=5, b=GB)

        def l3(s, kind, b):
            lo = (kind * GB + b) * E
            return Y[s][:, lo:lo + E]

        def seg(s, i):
            lo = 4 * GB * E + i * E
            return Y[s][0:HR, lo:lo + E]

        block = ctx.enter_context(nc.Block())

        @block.sync
        def _(sync):
            x_v = t["x"].rearrange("(g b) (a p) d -> g p a b d", b=GB, p=P)
            out_v = out.rearrange("(g b) (a p) d -> g p a b d", b=GB, p=P)

            def load(s, group):
                for a in range(NB):
                    sync.dma_start(X[s][:, a, :, :], x_v[group, :, a, :, :]).then_inc(x_loaded[s], 16)

            def load_weights(what):
                for dst, src in loads[what]:
                    sync.dma_start(dst, src, allow_slow_non_contiguous=True).then_inc(loaded[what], 16)

            def store(s, turn):
                sync.wait_ge(act_done[s], after(act_steps, turn, "x3", NB * GB // 2 - 1))
                sync.wait_ge(dve_done[s], after(dve_steps, turn, "x3", NB * GB // 2 - 1))
                for a in range(NB):
                    sync.dma_start(out_v[turn * STREAMS + s, :, a, :, :], F[s][:, a, :, :]).then_inc(y_stored[s], 16)

            load_weights("adj")
            load(0, 0)
            load_weights("w0")
            load_weights("w")
            load_weights("ends")
            sync.wait_ge(w_dve_done, after(w_dve_steps, 0, "done"))
            load(1, 1)
            with sync.Fori(0, TURNS - 1) as turn:
                for s in range(STREAMS):
                    sync.wait_ge(dve_done[s], after(dve_steps, turn, "y3", NB - 1))
                    load(s, turn * STREAMS + (STREAMS + s))
                    store(s, turn)
            for s in range(STREAMS):
                store(s, TURNS - 1)
            for s in range(STREAMS):
                sync.wait_ge(y_stored[s], (TURNS + 1) * 16 * NB)

        @block.gpsimd
        def _(gp):
            g = nc.gpsimd
            n = 0

            def link(ins):
                nonlocal n
                n += 1
                ins.then_inc(pool_chain, 1)
                gp.wait_ge(pool_chain, n)

            link(g.memset(ident[:, :], 0.0))
            link(g.affine_select(out=ident[:, :], in_=ident[:, :], compare_op=ALU.not_equal, fill=1.0, base=0,
                                 pattern=[[-1, P]], channel_multiplier=1))
            link(g.memset(ones[:, :], 1.0))
            link(g.memset(minus_half[:, :], -0.5))
            link(g.memset(head_of[:, :, :], 0.0))
            link(g.affine_select(out=head_of[:, :, :].rearrange("p b (h d) -> p b h d", h=HEADS),
                                 in_=head_of[:, :, :].rearrange("p b (h d) -> p b h d", h=HEADS),
                                 compare_op=ALU.not_equal, fill=1.0, base=0,
                                 pattern=[[-HEADS, GB], [-1, HEADS], [0, DH]], channel_multiplier=1))
            link(g.iota(node_row, pattern=[[1, N]], base=0, channel_multiplier=0,
                        allow_small_or_imprecise_dtypes=True))
            link(g.iota(node_col, pattern=[[P, NB]], base=0, channel_multiplier=1,
                        allow_small_or_imprecise_dtypes=True))
            for s in range(STREAMS):
                g.memset(small[s][:, 7, :], 0.0).then_inc(y_stored[s], 16 * NB)
            g.memset(a_pad[:, :], 0.0).then_inc(w_pool_done, 1)

            def low_part(s, lo, whole, hi):
                g.tensor_tensor(lo, whole, raw(hi), ALU.subtract).then_inc(pool_done[s], 1)

            def x0(turn, s):
                gp.wait_ge(x_loaded[s], (turn + 1) * (16 * NB))
                for a in range(NB):
                    gp.wait_ge(act_done[s], after(act_steps, turn, "x0_hi", a))
                    low_part(s, ZL[s][:, a, :, :], X[s][:, a, :, :], ZH[s][:, a, :, :])

            def neigh1(turn, s):
                for b in range(GB):
                    gp.wait_ge(act_done[s], after(act_steps, turn, "neigh1_hi", b))
                    low_part(s, ZL[s][:, :, b, :], y4(s, b), ZH[s][:, :, b, :])

            def conv1(turn, s):
                for b in range(GB):
                    gp.wait_ge(act_done[s], after(act_steps, turn, "h1_hi", b))
                    low_part(s, TL[s][:, b, :], h1(s, b), TH[s][:, b, :])

            def stats_of(turn, s, i):
                sm = small[s]
                gp.wait_ge(dve_done[s], after(dve_steps, turn, f"mean{i}"))
                g.tensor_tensor(sm[:, 6, :], sm[:, 5, :], minus_half[:, :], ALU.pow).then_inc(pool_done[s], 1)
                gp.wait_ge(pool_done[s], after(pool_steps, turn, f"rstd{i}"))
                g.tensor_tensor(sm[:, 0, :], sm[:, 6, :], sm[:, 7, :], ALU.mult).then_inc(pool_done[s], 1)

            def split_state(turn, s, k):
                for a in range(NB):
                    gp.wait_ge(act_done[s], after(act_steps, turn, f"euler{k}_hi", a))
                    low_part(s, z2(ZL[s], a), state(s, k, a), z2(ZH[s], a))

            def euler(turn, s, k):
                if k > 0:
                    split_state(turn, s, k)

            def x3(turn, s):
                for a in range(NB // 2):
                    gp.wait_ge(act_done[s], after(act_steps, turn, "x3_hi", a))
                    low_part(s, ZL[s][:, a, :, :], X[s][:, a, :, :], ZH[s][:, a, :, :])

            def w_one_hot():
                gp.wait_ge(w_dve_done, after(w_dve_steps, 0, "src_col"))
                for a in range(NB):
                    link(g.tensor_scalar(one_src[:, a, :], raw(ends_row[:, 0:E]), node_col[:, a:a + 1], None,
                                         ALU.is_equal))
                    link(g.tensor_scalar(E1[:, a, E:2 * E], raw(ends_row[:, E:2 * E]), node_col[:, a:a + 1], None,
                                         ALU.is_equal))
                    link(g.tensor_tensor(E1[:, a, 0:E], raw(one_src[:, a, :]), raw(E1[:, a, E:2 * E]), ALU.add))
                for e in range(EB):
                    link(g.tensor_scalar(S1[:, e, :], node_row, src_col[:, e:e + 1], None, ALU.is_equal))
                g.memset(pool_junk, 0.0).then_inc(w_pool_done, 1)

            def w_q():
                for factor in factors:
                    link(g.tensor_scalar(ident_by[factor], ident[:, :], factor, None, ALU.mult))
                g.memset(pool_junk, 0.0).then_inc(w_pool_done, 1)

            def w_end():
                gp.wait_ge(w_dve_done, after(w_dve_steps, 0, "done"))
                gp.wait_ge(w_act_done, after(w_act_steps, 0, "q_t", LOTS - 1))

            stages = {"x0": x0, "neigh1": neigh1, "conv1": conv1, "stats": stats_of, "split": split_state,
                      "euler": euler,
                      "x3": x3, "one_hot": w_one_hot, "q": w_q, "end": w_end}
            run(stages, prepare, 0)
            with gp.Fori(0, TURNS - 1) as turn:
                run(stages, in_turn, turn)
            run(stages, last_turn, TURNS - 1)

        @block.scalar
        def _(ac):
            A = nc.scalar

            def copy(out_, in_, **more):
                return A.activation(out_, in_, ACT.Copy, **more)

            def w_adj():
                for a in range(NB):
                    ac.wait_ge(w_pe_done, after(w_pe_steps, 0, "b_t", a))
                    copy(BTH[:, :, a * P:(a + 1) * P],
                         w_bank[a][:, :].rearrange("p (m n) -> p m n", n=P)).then_inc(w_act_done, 1)

            def w_low():
                for a in range(NB):
                    ac.wait_ge(w_dve_done, after(w_dve_steps, 0, "b_lo", a))
                    if a > 0:
                        ac.wait_ge(w_act_done, after(w_act_steps, 0, "low_sum", a - 1))
                    A.activation(rest_abs, raw(b_lo[:, a, :]), ACT.Abs,
                                 accum_out=low_sum[:, a:a + 1]).then_inc(w_act_done, 1)
                    ac.wait_ge(w_pe_done, after(w_pe_steps, 0, "b_lo_t", a))
                    copy(BTL[:, :, a * P:(a + 1) * P],
                         w_bank[(a + 1) % 4][:, :].rearrange("p (m n) -> p m n", n=P)).then_inc(w_act_done, 1)

            def w_v():
                ac.wait_ge(loaded["w"], 16 * len(loads["w"]))
                A.activation(tmp_a, alpha, ACT.Exp, scale=-1.0).then_inc(w_act_done, 1)
                ac.wait_ge(w_pe_done, after(w_pe_steps, 0, "w_t"))
                copy(w_t[:, 0, :], w_bank[2][:, 0:D]).then_inc(w_act_done, 1)

            def w_picked():
                ac.wait_ge(w_dve_done, after(w_dve_steps, 0, "log_in"))
                A.activation(log_a[:, :], log_a[:, :], ACT.Ln).then_inc(w_act_done, 1)

            def w_soft():
                for a in range(NB):
                    ac.wait_ge(w_dve_done, after(w_dve_steps, 0, "rowmax", a))
                    A.activation(soft, soft, ACT.Exp, bias=tmp_b[:, a:a + 1],
                                 accum_out=tmp_c[:, a:a + 1]).then_inc(w_act_done, 1)

            def w_q():
                for i in range(LOTS):
                    ac.wait_ge(w_pe_done, after(w_pe_steps, 0, "q_t", i))
                    copy(QH[:, i * LOT:(i + 1) * LOT, :], w_bank[i][:, 0:LOT * D]).then_inc(w_act_done, 1)
                ac.wait_ge(w_dve_done, after(w_dve_steps, 0, "done"))

            def from_psum(turn, s, stage, i, out_, part=None, **more):
                ac.wait_ge(pe_done[s], after(pe_steps, turn, stage, i))
                src = bank[s][i % 4][:, :] if part is None else part
                copy(out_, src, **more).then_inc(act_done[s], 1)

            def x0(turn, s):
                ac.wait_ge(x_loaded[s], (turn + 1) * (16 * NB))
                for a in range(NB):
                    copy(ZH[s][:, a, :, :], X[s][:, a, :, :]).then_inc(act_done[s], 1)

            def t0(turn, s):
                for b in range(GB):
                    from_psum(turn, s, "t0", b, TH[s][:, b, :])

            def neigh1(turn, s):
                for b in range(GB):
                    ac.wait_ge(dve_done[s], after(dve_steps, turn, "neigh1", b))
                    copy(ZH[s][:, :, b, :], y4(s, b)).then_inc(act_done[s], 1)

            def conv1(turn, s):
                for b in range(GB):
                    ac.wait_ge(pe_done[s], after(pe_steps, turn, "conv1", b))
                    A.activation(h1(s, b), bank[s][b][:, :], ACT.Relu, bias=b1).then_inc(act_done[s], 1)
                    A.activation(TH[s][:, b, :], bank[s][b][:, :], ACT.Relu, bias=b1).then_inc(act_done[s], 1)

            def triple(turn, s):
                ac.wait_ge(pool_done[s], after(pool_steps, turn, "x0_lo", NB - 1))
                for a in range(NB):
                    copy(X[s][:, a, :, :], X[s][:, a, :, :], scale=3.0).then_inc(act_done[s], 1)

            def pair2(turn, s):
                for i in range(8):
                    a, pair = i % 4, i // 4
                    from_psum(turn, s, "pair2", i, ZH[s][:, a, 2 * pair:2 * pair + 2, :], half(s, i, 0))

            def t1(turn, s):
                for b in range(GB):
                    from_psum(turn, s, "t1", b, TH[s][:, b, :], bias=1.0)

            def lot(turn, s, l, a):
                if l:
                    ac.wait_ge(dve_done[s], after(dve_steps, turn, f"euler{lots[l][1][0] + 1}", NB - 1))
                for b in range(GB):
                    i = a * GB + b
                    from_psum(turn, s, f"lot{l}", i, y_terms(s)[:, :, a, b, :],
                              bank[s][i % 4][:, 0:LOT * D].rearrange("p (k d) -> p k d", d=D))

            def split_state(turn, s, k):
                if k < EULER_STEPS:
                    ac.wait_ge(pe_done[s], after(pe_steps, turn, f"euler{k}", NB - 1))
                for a in range(NB):
                    if k < EULER_STEPS:
                        ac.wait_ge(dve_done[s], after(dve_steps, turn, f"euler{k}", a))
                    else:
                        ac.wait_ge(act_done[s], after(act_steps, turn, "lot0", a * GB + GB - 1))
                    copy(z2(ZH[s], a), state(s, k, a)).then_inc(act_done[s], 1)

            def euler(turn, s, k):
                if k > 0:
                    split_state(turn, s, k)

            def t2(turn, s):
                for b in range(GB):
                    from_psum(turn, s, "t2", b, TH[s][:, b, :], bias=1.0)

            def l2(turn, s, a):
                if a >= 2:
                    ac.wait_ge(dve_done[s], after(dve_steps, turn, "l2_sum3", a - 2))
                for i in range(2 * GB * a, 2 * GB * (a + 1)):
                    b, j = i // 2 % GB, i % 2
                    n = (3, 2)[j]
                    from_psum(turn, s, "l2", i, terms2(s, a)[:, 3 * j:3 * j + n, b, :],
                              bank[s][i % 4][:, 0:n * D].rearrange("p (k d) -> p k d", d=D))

            def x3(turn, s):
                ac.wait_ge(dve_done[s], after(dve_steps, turn, "x2", NB * GB // 2 - 1))
                ac.wait_ge(act_done[s], after(act_steps, turn, "x2", NB * GB // 2 - 1))
                for a in range(NB):
                    copy(ZH[s][:, a, :, :], X[s][:, a, :, :]).then_inc(act_done[s], 1)

            def gather(turn, s):
                for b in range(GB):
                    from_psum(turn, s, "gather", b, TH[s][:, b, :])

            def qv(turn, s):
                for b in range(GB):
                    from_psum(turn, s, "qv", b, l3(s, 0, b), bank[s][b][:, 0:E])
                for b in range(GB):
                    copy(l3(s, 2, b), bank[s][b][:, E:2 * E]).then_inc(act_done[s], 1)

            def score(turn, s):
                ac.wait_ge(dve_done[s], after(dve_steps, turn, "seg", 2))
                A.activation(seg(s, 3), seg(s, 2), ACT.Exp).then_inc(act_done[s], 1)

            def wout(turn, s):
                for b in range(GB):
                    from_psum(turn, s, "wout", b, ZH[s][:, 0:EB, b, :],
                              bank[s][b][:, 0:EB * D].rearrange("p (k d) -> p k d", d=D))

            def norm(turn, s, i):
                src, sm = (X if i == 0 else F), small[s]
                to = F if i == 3 else X
                ac.wait_ge(pool_done[s], after(pool_steps, turn, f"shift{i}"))
                for c in range(NB * GB // 2):
                    b, a = divmod(c, NB)
                    at_c = a * GB + b
                    A.activation(to[s][:, a, b, :], src[s][:, a, b, :], ACT.Identity, bias=sm[:, 0, at_c:at_c + 1],
                                 scale=sm[:, 6, at_c:at_c + 1]).then_inc(act_done[s], 1)

            stages = {"adj": w_adj, "low": w_low, "v": w_v, "picked": w_picked, "soft": w_soft, "end": w_q,
                      "norm": norm, "x0": x0, "t0": t0, "neigh1": neigh1, "conv1": conv1, "triple": triple,
                      "pair2": pair2, "t1": t1,
                      "lot": lot, "split": split_state, "euler": euler,
                      "t2": t2, "l2": l2, "x3": x3, "gather": gather, "qv": qv, "score": score, "wout": wout}
            run(stages, prepare, 0)
            with ac.Fori(0, TURNS - 1) as turn:
                run(stages, in_turn, turn)
            run(stages, last_turn, TURNS - 1)

        @block.vector
        def _(dv):
            v = nc.vector
            n = 0

            def link(ins):
                nonlocal n
                n += 1
                ins.then_inc(dve_chain, 1)
                dv.wait_ge(dve_chain, n)

            def split(hi, lo, whole):
                link(v.tensor_copy(hi, whole))
                link(v.tensor_tensor(lo, whole, raw(hi), ALU.subtract))

            def w_adj():
                dv.wait_ge(loaded["adj"], 16)
                link(v.tensor_reduce(r, adj_sb, AX, ALU.max))
                link(v.tensor_reduce(tmp_b, adj_sb, AX, ALU.min))
                link(v.scalar_tensor_tensor(r, tmp_b, -1.0, r, ALU.mult, ALU.max))
                link(v.tensor_scalar(r, r, 1e-30, None, ALU.max))
                link(v.reciprocal(r_inv, r))
                for a in range(NB):
                    v.tensor_scalar(b_hi[:, a, :], adj_sb[:, a, :], r_inv[:, a:a + 1], None,
                                    ALU.mult).then_inc(w_dve_done, 1)
                dv.wait_ge(w_pool_done, after(w_pool_steps, 0, "const"))
                for a in range(NB):
                    link(v.tensor_scalar(r_diag[:, a * P:(a + 1) * P], ident[:, :], r[:, a:a + 1], None, ALU.mult))
                v.tensor_scalar(neg_r, r, -1.0, None, ALU.mult).then_inc(w_dve_done, 1)

            def w_low():
                dv.wait_ge(w_dve_done, after(w_dve_steps, 0, "r_diag"))
                for a in range(NB):
                    link(v.scalar_tensor_tensor(rest, raw(b_hi[:, a, :]), neg_r[:, a:a + 1], adj_sb[:, a, :],
                                                ALU.mult, ALU.add))
                    v.tensor_scalar(b_lo[:, a, :], rest, r_inv[:, a:a + 1], None, ALU.mult).then_inc(w_dve_done, 1)
                    dv.wait_ge(w_dve_done, after(w_dve_steps, 0, "b_lo", a))
                dv.wait_ge(w_pe_done, after(w_pe_steps, 0, "r_row"))
                v.tensor_copy(r_row[:, :], w_bank[0][:, :]).then_inc(w_dve_done, 1)

            def w_w0():
                dv.wait_ge(loaded["w0"], 16 * len(loads["w0"]))
                split(w1H[:, :, :], w1L[:, :, :], w_in[:, W1N:W1L + 1, :])
                w2_in = w_in[:, W2N:W2L + 1, :].rearrange("p a d -> p (a d)")
                split(w2H[:, :], w2L[:, :], w2_in)
                dv.wait_ge(w_pe_done, after(w_pe_steps, 0, "low"))
                v.tensor_scalar(inexact[:, :], w_bank[1][0:1, 0:1], 0.0, None, ALU.is_gt).then_inc(w_dve_done, 1)

            def w_v():
                dv.wait_ge(loaded["w"], 16 * len(loads["w"]))
                dv.wait_ge(w_act_done, after(w_act_steps, 0, "sigmoid"))
                link(v.tensor_scalar(tmp_a, tmp_a, 1.0, None, ALU.add))
                link(v.reciprocal(tmp_a, tmp_a))
                link(v.tensor_scalar(c_neg, tmp_a, -0.5 * DT, None, ALU.mult))
                link(v.scalar_tensor_tensor(c_r, c_neg, -1.0, r, ALU.mult, ALU.mult))
                link(v.tensor_scalar(d_col, d_col, 0.0, 1.0, ALU.max, ALU.min))
                dv.wait_ge(w_act_done, after(w_act_steps, 0, "w_t"))
                v.tensor_scalar(w_t[:, 1, :], w_t[:, 0, :], d_col, None, ALU.mult).then_inc(w_dve_done, 1)
                link(v.tensor_scalar(ident_v, ident[:, :], 1.0 - DT, None, ALU.mult))
                dv.wait_ge(w_pe_done, after(w_pe_steps, 0, "w_eff"))
                v.scalar_tensor_tensor(V, w_bank[3][:, 0:D], DT, ident_v, ALU.mult, ALU.add).then_inc(w_dve_done, 1)
                link(v.tensor_reduce(mean_col, w_in[:, FC, :], AX, ALU.add))
                link(v.tensor_tensor(shift_col, fcb_col, mean_col, ALU.subtract))
                link(v.tensor_scalar(shift_col, shift_col, 1.0 / D, None, ALU.mult))
                link(v.tensor_scalar(power(0, 0), w_in[:, FC, :], shift_col, None, ALU.add))
                v.tensor_scalar(power(0, 1), ident[:, :], -1.0 / D, None, ALU.add).then_inc(w_dve_done, 1)
                dv.wait_ge(w_pe_done, after(w_pe_steps, 0, "nv1_t"))
                v.tensor_copy(nv1_t, w_bank[0][0:RANK, :]).then_inc(w_dve_done, 1)

            def w_edges():
                dv.wait_ge(loaded["ends"], 16 * len(loads["ends"]))
                link(v.tensor_copy(ends_col, ends_col_i))
                link(v.tensor_copy(ends_row, ends_row_i))
                link(v.scalar_tensor_tensor(key_row, raw(ends_row[:, 0:E]), float(E), node_row[:, 0:E],
                                            ALU.mult, ALU.add))
                link(v.scalar_tensor_tensor(key_col, ends_col[:, 0:EB], float(E), node_col[:, 0:EB],
                                            ALU.mult, ALU.add))
                for e in range(EB):
                    link(v.tensor_scalar(less, key_row, key_col[:, e:e + 1], None, ALU.is_lt, ALU.add,
                                         accum_out=rank[:, e:e + 1]))
                    link(v.tensor_scalar(perm[:, e, :], node_row[:, 0:E], rank[:, e:e + 1], None, ALU.is_equal))
                    for side in range(2):
                        link(v.tensor_scalar(perm_ends[:, e, side * E:(side + 1) * E], raw(perm[:, e, :]),
                                             ends_col[:, side * EB + e:side * EB + e + 1], None, ALU.mult))
                v.memset(tmp_c, 0.0).then_inc(w_dve_done, 1)
                dv.wait_ge(w_pe_done, after(w_pe_steps, 0, "ends_row"))
                v.tensor_copy(ends_row, w_bank[1][:, :]).then_inc(w_dve_done, 1)
                dv.wait_ge(w_pe_done, after(w_pe_steps, 0, "src_col"))
                v.tensor_copy(src_col, w_bank[2][:, 0:EB]).then_inc(w_dve_done, 1)

            def w_one_hot():
                dv.wait_ge(w_dve_done, after(w_dve_steps, 0, "src_col"))
                link(v.memset(edge[:, 0, :], 1.0))
                link(v.tensor_tensor(edge[:, 0, 1:E], raw(ends_row[0:HR, 1:E]), raw(ends_row[0:HR, 0:E - 1]),
                                     ALU.not_equal))
                link(v.tensor_scalar(edge[:, 1, :], edge[:, 0, :], -BIG, None, ALU.mult))
                link(v.tensor_scalar(edge[:, 2, :], edge[:, 0, :], -1.0, 1.0, ALU.mult, ALU.add))
                v.memset(tmp_c, 0.0).then_inc(w_dve_done, 1)
                link(v.tensor_tensor(w_sum[:, 0, :], w_l2[:, 0, :], ident[:, :], ALU.add))
                link(v.tensor_tensor(w_sum[:, 1, :], w_l2[:, 1, :], w_l2[:, 3, :], ALU.add))
                link(v.tensor_tensor(w_sum[:, 2, :], w_l2[:, 2, :], w_l2[:, 4, :], ALU.add))
                v.tensor_copy(w_sum[:, 3:5, :], w_l2[:, 5:7, :]).then_inc(w_dve_done, 1)

            def w_powers():
                for i, (out_, j, width) in enumerate(((power_1, 3, 3 * D), (powers[:, 0, :], 0, 4 * D),
                                                      (V4, 3, D), (powers[:, 1, :], 0, 4 * D),
                                                      (powers[:, 2, :], 3, 4 * D), (last_power, 0, D))):
                    dv.wait_ge(w_pe_done, after(w_pe_steps, 0, "power", i))
                    src = w_bank[j][:, 0:width]
                    if i == 0:
                        src = src.rearrange("p (a d) -> p a d", d=D)
                    v.tensor_copy(out_, src).then_inc(w_dve_done, 1)

            def w_weights():
                dv.wait_ge(w_pe_done, after(w_pe_steps, 0, "l2_mean", 1))
                dv.wait_ge(w_dve_done, after(w_dve_steps, 0, "l2_sum"))
                link(v.scalar_tensor_tensor(w_sum[:, 0:4, :], w_bank[1][:, :].rearrange("p (j d) -> p j d", d=D),
                                            -1.0 / D, w_sum[:, 0:4, :], ALU.mult, ALU.add))
                v.scalar_tensor_tensor(w_sum[:, 4, :], w_bank[2][:, 0:D], -1.0 / D, w_sum[:, 4, :],
                                       ALU.mult, ALU.add).then_inc(w_dve_done, 1)
                dv.wait_ge(w_dve_done, after(w_dve_steps, 0, "l2_w"))
                link(v.scalar_tensor_tensor(w_sum[:, 0, :], b_l2, 1.0 / D, w_sum[:, 0, :], ALU.mult, ALU.add))
                split(VH[:, :, :], VL[:, :, :], w_sum)
                dv.wait_ge(w_pe_done, after(w_pe_steps, 0, "g_t"))
                link(v.tensor_copy(w_t, w_bank[3][:, 0:2 * D].rearrange("p (a d) -> p a d", d=D)))
                split(gH[:, :, :], gL[:, :, :], w_t)
                link(v.tensor_copy(w_out[:, :], w_bank[3][:, 2 * D:3 * D]))
                for h in range(HEADS):
                    at_h = HR - HEADS + h
                    link(v.tensor_copy(a_pad[h * DH:(h + 1) * DH, at_h:at_h + 1], a_col[h * DH:(h + 1) * DH, :]))
                v.tensor_reduce(row_sum, adj_sb, AX, ALU.add).then_inc(w_dve_done, 1)

            def w_picked():
                dv.wait_ge(w_pool_done, after(w_pool_steps, 0, "one_hot"))
                for a in range(NB):
                    dv.wait_ge(w_pe_done, after(w_pe_steps, 0, "adj_rows", a))
                    v.tensor_tensor(picked[:, a, :], w_bank[1 + a % 2][:, 0:E], raw(E1[:, a, E:2 * E]),
                                    ALU.mult).then_inc(w_dve_done, 1)
                dv.wait_ge(w_pe_done, after(w_pe_steps, 0, "picked"))
                v.tensor_scalar(log_a[:, :], w_bank[3][0:1, 0:E], 1e-8, None, ALU.add).then_inc(w_dve_done, 1)

            def w_soft():
                for a in range(NB):
                    dv.wait_ge(w_pe_done, after(w_pe_steps, 0, "logits", a))
                    link(v.tensor_scalar(soft, w_bank[a % 2][:, :], 0.0, None, ALU.max, ALU.max,
                                         accum_out=tmp_a[:, a:a + 1]))
                    v.tensor_scalar(tmp_b[:, a:a + 1], tmp_a[:, a:a + 1], -1.0, None,
                                    ALU.mult).then_inc(w_dve_done, 1)
                    dv.wait_ge(w_act_done, after(w_act_steps, 0, "soft", a))
                    link(v.reciprocal(tmp_a[:, a:a + 1], tmp_c[:, a:a + 1]))
                    v.tensor_scalar(soft, soft, tmp_a[:, a:a + 1], None, ALU.mult, ALU.add,
                                    accum_out=t_sum[:, a:a + 1]).then_inc(w_dve_done, 1)
                    dv.wait_ge(w_dve_done, after(w_dve_steps, 0, "t_sum", a))

            def w_q():
                for i in range(LOTS):
                    dv.wait_ge(w_act_done, after(w_act_steps, 0, "q_t", i))
                    part = slice(i * LOT, (i + 1) * LOT)
                    link(v.tensor_tensor(QL[:, part, :],
                                         w_bank[i][:, 0:LOT * D].rearrange("p (k d) -> p k d", d=D),
                                         raw(QH[:, part, :]), ALU.subtract))
                v.memset(tmp_c, 0.0).then_inc(w_dve_done, 1)
                dv.wait_ge(w_dve_done, after(w_dve_steps, 0, "done"))

            def low(turn, s, stage, hi_step, i, lo, hi, part, shift=None):
                dv.wait_ge(pe_done[s], after(pe_steps, turn, stage, i))
                dv.wait_ge(act_done[s], after(act_steps, turn, hi_step, i))
                ins = (v.tensor_tensor(lo, part, raw(hi), ALU.subtract) if shift is None else
                       v.scalar_tensor_tensor(lo, part, shift, raw(hi), ALU.add, ALU.subtract))
                ins.then_inc(dve_done[s], 1)

            def block_stats(turn, s, i, a, what):
                src = X if i == 0 else F
                dv.wait_ge(dve_done[s], after(dve_steps, turn, what, a))
                for b in range(GB):
                    v.bn_stats(stats[s][:, a * GB + b, :], src[s][:, a, b, :]).then_inc(dve_done[s], 1)

            def stats_of(turn, s, i):
                eps = 4e-5 if i == 0 else 1e-5
                st, sm = stats[s], small[s]
                dv.wait_ge(dve_done[s], after(dve_steps, turn, f"stats{i}_{GB - 1}", NB - 1))
                v.tensor_tensor(sm[:, 0, :], st[:, :, 1], st[:, :, 4], ALU.add).then_inc(dve_done[s], 1)
                v.tensor_tensor(sm[:, 1, :], st[:, :, 1], st[:, :, 4], ALU.subtract).then_inc(dve_done[s], 1)
                v.tensor_tensor(sm[:, 2, :], st[:, :, 2], st[:, :, 5], ALU.add).then_inc(dve_done[s], 1)
                dv.wait_ge(dve_done[s], after(dve_steps, turn, f"half_difference{i}"))
                v.tensor_tensor(sm[:, 3, :], sm[:, 1, :], sm[:, 1, :], ALU.mult).then_inc(dve_done[s], 1)
                dv.wait_ge(dve_done[s], after(dve_steps, turn, f"square{i}"))
                v.scalar_tensor_tensor(sm[:, 4, :], sm[:, 3, :], D / 4.0, sm[:, 2, :],
                                       ALU.mult, ALU.add).then_inc(dve_done[s], 1)
                dv.wait_ge(dve_done[s], after(dve_steps, turn, f"spread{i}"))
                v.tensor_scalar(sm[:, 5, :], sm[:, 4, :], 1.0 / D, eps, ALU.mult, ALU.add).then_inc(dve_done[s], 1)
                v.tensor_scalar(sm[:, 7, :], sm[:, 0, :], -0.5, None, ALU.mult).then_inc(dve_done[s], 1)

            def norm(turn, s, i):
                src, sm = (X if i == 0 else F), small[s]
                to = F if i == 3 else X
                dv.wait_ge(pool_done[s], after(pool_steps, turn, f"rstd{i}"))
                for c in range(NB * GB // 2, NB * GB):
                    b, a = divmod(c, NB)
                    at_c = a * GB + b
                    v.tensor_scalar(to[s][:, a, b, :], src[s][:, a, b, :], sm[:, 7, at_c:at_c + 1],
                                    sm[:, 6, at_c:at_c + 1], ALU.add, ALU.mult).then_inc(dve_done[s], 1)

            def t0(turn, s):
                for b in range(GB):
                    low(turn, s, "t0", "t0_hi", b, TL[s][:, b, :], TH[s][:, b, :], bank[s][b][:, :])

            def neigh1(turn, s):
                for b in range(GB):
                    dv.wait_ge(pe_done[s], after(pe_steps, turn, "neigh1", b))
                    v.tensor_tensor(y4_flat(s, b), bank[s][b][:, :], r_row[:, :], ALU.mult).then_inc(dve_done[s], 1)

            def pair2(turn, s):
                dv.wait_ge(y_stored[s], (turn + 1) * (16 * NB))
                for i in range(8):
                    a, pair = i % 4, i // 4
                    two = slice(2 * pair, 2 * pair + 2)
                    low(turn, s, "pair2", "z2_hi", i, ZL[s][:, a, two, :], ZH[s][:, a, two, :], half(s, i, 0))
                    v.tensor_tensor(F[s][:, a, two, :], half(s, i, 1), b2_row[:, :, :],
                                    ALU.add).then_inc(dve_done[s], 1)

            def neigh2(turn, s):
                dv.wait_ge(dve_done[s], after(dve_steps, turn, "loop2", 7))
                for a in range(NB):
                    dv.wait_ge(pe_done[s], after(pe_steps, turn, "neigh2", a))
                    v.scalar_tensor_tensor(F[s][:, a, :, :], wide(s, a), r[:, a:a + 1], F[s][:, a, :, :],
                                           ALU.mult, ALU.add).then_inc(dve_done[s], 1)
                    dv.wait_ge(dve_done[s], after(dve_steps, turn, "conv2", a))
                    dv.wait_ge(act_done[s], after(act_steps, turn, "x_3", a))
                    v.scalar_tensor_tensor(X[s][:, a, :, :], F[s][:, a, :, :], 0.0, X[s][:, a, :, :],
                                           ALU.max, ALU.add).then_inc(dve_done[s], 1)
                    block_stats(turn, s, 0, a, "y0")

            def t1(turn, s):
                for b in range(GB):
                    low(turn, s, "t1", "t1_hi", b, TL[s][:, b, :], TH[s][:, b, :], bank[s][b][:, :], 1.0)

            def local(turn, s, k):
                l, i_k = divmod(EULER_STEPS - k, LOT)
                if k < EULER_STEPS - 1:
                    dv.wait_ge(dve_done[s], after(dve_steps, turn, f"euler{k + 1}", NB - 1))
                for a in range(NB):
                    dv.wait_ge(act_done[s], after(act_steps, turn, f"lot{l}", a * GB + GB - 1))
                    term = y_terms(s)[:, i_k, a, :, :]
                    v.scalar_tensor_tensor(term, state(s, k + 1, a), c_neg[:, a:a + 1], term,
                                           ALU.mult, ALU.add).then_inc(dve_done[s], 1)

            def euler(turn, s, k):
                i_k = (EULER_STEPS - k) % LOT
                for a in range(NB):
                    dv.wait_ge(dve_done[s], after(dve_steps, turn, f"local{k}", a))
                    dv.wait_ge(pe_done[s], after(pe_steps, turn, f"euler{k}", a))
                    term = y_terms(s)[:, i_k, a, :, :]
                    v.scalar_tensor_tensor(F[s][:, a, :, :], wide(s, a), c_r[:, a:a + 1], term,
                                           ALU.mult, ALU.add).then_inc(dve_done[s], 1)
                    if k == 0:
                        block_stats(turn, s, 1, a, "euler0")

            def t2(turn, s):
                for b in range(GB):
                    low(turn, s, "t2", "t2_hi", b, TL[s][:, b, :], TH[s][:, b, :], bank[s][b][:, :], 1.0)

            def l2(turn, s, a):
                dv.wait_ge(act_done[s], after(act_steps, turn, "l2", 8 * a + 7))
                A = [terms2(s, a)[:, j, :, :] for j in range(5)]
                s_a, t_a = row_sum[:, a:a + 1], t_sum[:, a:a + 1]
                stt = v.scalar_tensor_tensor
                stt(A[1], A[2], s_a, A[1], ALU.mult, ALU.add).then_inc(dve_done[s], 1)
                stt(A[3], A[4], t_a, A[3], ALU.mult, ALU.add).then_inc(dve_done[s], 1)
                dv.wait_ge(dve_done[s], after(dve_steps, turn, "l2_sum0", a))
                stt(A[0], A[1], s_a, A[0], ALU.mult, ALU.add).then_inc(dve_done[s], 1)
                dv.wait_ge(dve_done[s], after(dve_steps, turn, "l2_sum2", a))
                stt(F[s][:, a, :, :], A[3], t_a, A[0], ALU.mult, ALU.add).then_inc(dve_done[s], 1)
                block_stats(turn, s, 2, a, "l2_sum3")

            def x3(turn, s):
                for a in range(NB // 2, NB):
                    dv.wait_ge(act_done[s], after(act_steps, turn, "x3_hi", a))
                    v.tensor_tensor(ZL[s][:, a, :, :], X[s][:, a, :, :], raw(ZH[s][:, a, :, :]),
                                    ALU.subtract).then_inc(dve_done[s], 1)

            def gather(turn, s):
                for b in range(GB):
                    low(turn, s, "gather", "gather_hi", b, TL[s][:, b, :], TH[s][:, b, :], bank[s][b][:, :])

            def qv(turn, s):
                for b in range(GB):
                    dv.wait_ge(act_done[s], after(act_steps, turn, "q", b))
                    v.scalar_tensor_tensor(l3(s, 1, b), l3(s, 0, b), 0.2, l3(s, 0, b), ALU.mult,
                                           ALU.max).then_inc(dve_done[s], 1)

            def score(turn, s):
                first, last = slice(0, E), slice(1, E + 1)
                back = slice(None, None, -1)
                scores = bank[s][0][0:HR, 0:E]
                dv.wait_ge(pe_done[s], after(pe_steps, turn, "score"))
                v.tensor_tensor_scan(seg(s, 0), edge[:, 1, first], scores, 0.0,
                                     ALU.add, ALU.max).then_inc(dve_done[s], 1)
                dv.wait_ge(dve_done[s], after(dve_steps, turn, "seg", 0))
                v.tensor_tensor_scan(seg(s, 1)[:, back], edge[:, 1, last][:, back], seg(s, 0)[:, back], 0.0,
                                     ALU.add, ALU.max).then_inc(dve_done[s], 1)
                dv.wait_ge(dve_done[s], after(dve_steps, turn, "seg", 1))
                v.tensor_tensor(seg(s, 2), scores, seg(s, 1), ALU.subtract).then_inc(dve_done[s], 1)
                dv.wait_ge(act_done[s], after(act_steps, turn, "exp"))
                v.tensor_tensor_scan(seg(s, 4), edge[:, 2, first], seg(s, 3), 0.0,
                                     ALU.mult, ALU.add).then_inc(dve_done[s], 1)
                dv.wait_ge(dve_done[s], after(dve_steps, turn, "seg", 3))
                v.tensor_tensor_scan(seg(s, 5)[:, back], edge[:, 2, last][:, back], seg(s, 4)[:, back], 0.0,
                                     ALU.mult, ALU.max).then_inc(dve_done[s], 1)
                dv.wait_ge(dve_done[s], after(dve_steps, turn, "seg", 4))
                v.reciprocal(seg(s, 6), seg(s, 5)).then_inc(dve_done[s], 1)
                dv.wait_ge(dve_done[s], after(dve_steps, turn, "seg", 5))
                v.tensor_tensor(seg(s, 7), seg(s, 3), seg(s, 6), ALU.mult).then_inc(dve_done[s], 1)

            def spread(turn, s):
                for b in range(GB):
                    dv.wait_ge(pe_done[s], after(pe_steps, turn, "spread", b))
                    dv.wait_ge(act_done[s], after(act_steps, turn, "v", b))
                    v.tensor_tensor(l3(s, 3, b), bank[s][b][:, 0:E], l3(s, 2, b), ALU.mult).then_inc(dve_done[s], 1)

            def wout(turn, s):
                for b in range(GB):
                    low(turn, s, "wout", "wout_hi", b, ZL[s][:, 0:EB, b, :], ZH[s][:, 0:EB, b, :],
                        bank[s][b][:, 0:EB * D].rearrange("p (k d) -> p k d", d=D))

            def scatter(turn, s):
                for a in range(NB):
                    dv.wait_ge(pe_done[s], after(pe_steps, turn, "scatter", a))
                    v.tensor_tensor(F[s][:, a, :, :], wide(s, a), X[s][:, a, :, :], ALU.add).then_inc(dve_done[s], 1)
                    block_stats(turn, s, 3, a, "y3")

            stages = {"adj": w_adj, "low": w_low, "w0": w_w0, "v": w_v, "edges": w_edges, "one_hot": w_one_hot,
                      "powers": w_powers, "weights": w_weights, "picked": w_picked, "soft": w_soft, "end": w_q,
                      "t0": t0, "neigh1": neigh1, "pair2": pair2, "neigh2": neigh2, "stats": stats_of,
                      "norm": norm, "t1": t1,
                      "local": local, "euler": euler, "t2": t2, "l2": l2, "x3": x3, "gather": gather, "qv": qv,
                      "score": score, "spread": spread, "wout": wout, "scatter": scatter}
            run(stages, prepare, 0)
            with dv.Fori(0, TURNS - 1) as turn:
                run(stages, in_turn, turn)
            run(stages, last_turn, TURNS - 1)

        @block.tensor
        def _(pt):
            T = nc.tensor

            def products(out_, terms):
                for n, (lhs_t, rhs) in enumerate(terms):
                    last = T.matmul(out_, lhs_t, rhs, start=n == 0, stop=n == len(terms) - 1)
                return last

            def three(lh, ll, rh, rl):
                return [(lh, rh), (lh, rl), (ll, rh)]

            def block_of(i, width=P):
                return slice(i * width, (i + 1) * width)

            has_low = None

            def w_adj():
                pt.wait_ge(w_pool_done, after(w_pool_steps, 0, "const"))
                for a in range(NB):
                    pt.wait_ge(w_dve_done, after(w_dve_steps, 0, "b_hi", a))
                    for m in range(NB):
                        last = T.transpose(w_bank[a][:, block_of(m)], raw(b_hi[:, a, block_of(m)]), ident[:, :])
                    last.then_inc(w_pe_done, 1)
                pt.wait_ge(w_dve_done, after(w_dve_steps, 0, "r_diag"))
                pt.wait_ge(w_act_done, after(w_act_steps, 0, "b_t", 0))
                products(w_bank[0][:, :], [(ones[:, :], r_diag)]).then_inc(w_pe_done, 1)

            def w_low():
                for a in range(NB):
                    if a < NB - 1:
                        pt.wait_ge(w_act_done, after(w_act_steps, 0, "b_t", a + 1))
                        pt.wait_ge(w_dve_done, after(w_dve_steps, 0, "b_lo", a))
                    else:
                        pt.wait_ge(w_dve_done, after(w_dve_steps, 0, "r_row"))
                    for m in range(NB):
                        last = T.transpose(w_bank[(a + 1) % 4][:, block_of(m)], raw(b_lo[:, a, block_of(m)]),
                                           ident[:, :])
                    last.then_inc(w_pe_done, 1)
                pt.wait_ge(w_act_done, after(w_act_steps, 0, "low_sum", NB - 1))
                products(w_bank[1][0:1, 0:1], [(ones[:, 0:1], low_sum[:, a:a + 1])
                                               for a in range(NB)]).then_inc(w_pe_done, 1)

            def w_w0():
                nonlocal has_low
                pt.wait_ge(w_dve_done, after(w_dve_steps, 0, "inexact"))
                has_low = pt.value_load(inexact[0:1, 0:1])

            def w_v():
                pt.wait_ge(loaded["w"], 16 * len(loads["w"]))
                pt.wait_ge(w_act_done, after(w_act_steps, 0, "b_lo_t", NB - 1))
                T.transpose(w_bank[2][:, 0:D], w_in[:, WE, :], ident[:, :]).then_inc(w_pe_done, 1)
                pt.wait_ge(w_dve_done, after(w_dve_steps, 0, "w_by_d"))
                products(w_bank[3][:, 0:D], [(w_t[:, 1, :], w_t[:, 0, :])]).then_inc(w_pe_done, 1)
                for a in range(NB):
                    last = T.transpose(w_bank[0][0:RANK, block_of(a)], nv1[:, a, :], ident[:, :])
                last.then_inc(w_pe_done, 1)

            def w_edges():
                pt.wait_ge(w_dve_done, after(w_dve_steps, 0, "perm"))
                products(w_bank[1][:, :], [(ones[:, :], raw(perm_ends[:, e, :]))
                                         for e in range(EB)]).then_inc(w_pe_done, 1)
                for e in range(EB):
                    last = products(w_bank[2][:, e:e + 1], [(raw(perm[:, f, block_of(e)]), ends_col[:, f:f + 1])
                                                            for f in range(EB)])
                last.then_inc(w_pe_done, 1)

            def w_powers():
                products(w_bank[3][:, 0:3 * D], [(V, power_0)]).then_inc(w_pe_done, 1)
                pt.wait_ge(w_dve_done, after(w_dve_steps, 0, "power", 0))
                for p in range(2):
                    last = products(w_bank[0][:, block_of(p, 2 * D)], [(V2, (power_0, power_1)[p][:, 1:3, :])])
                last.then_inc(w_pe_done, 1)
                products(w_bank[3][:, 0:D], [(V2, V2)]).then_inc(w_pe_done, 1)
                pt.wait_ge(w_dve_done, after(w_dve_steps, 0, "power", 2))
                for p in range(2):
                    last = products(w_bank[0][:, block_of(p, 2 * D)], [(V4, (power_0, power_1)[p][:, 1:3, :])])
                last.then_inc(w_pe_done, 1)
                products(w_bank[3][:, :], [(V4, powers[:, 0, :])]).then_inc(w_pe_done, 1)
                pt.wait_ge(w_dve_done, after(w_dve_steps, 0, "power", 3))
                products(w_bank[0][:, 0:D], [(V4, power(4, 0))]).then_inc(w_pe_done, 1)

            def w_l2():
                pt.wait_ge(w_dve_done, after(w_dve_steps, 0, "l2_sum"))
                products(w_bank[1][:, :], [(ones[:, :], w_sum[:, 0:4, :])]).then_inc(w_pe_done, 1)
                products(w_bank[2][:, 0:D], [(ones[:, :], w_sum[:, 4, :])]).then_inc(w_pe_done, 1)

            def w_weights():
                pt.wait_ge(w_dve_done, after(w_dve_steps, 0, "power", 4))
                for i, w in enumerate((WLIN, WVAL, WOUT)):
                    last = T.transpose(w_bank[3][:, block_of(i)], w_in[:, w, :], ident[:, :])
                last.then_inc(w_pe_done, 1)

            def w_picked():
                pt.wait_ge(w_dve_done, after(w_dve_steps, 0, "l2_w"))
                pt.wait_ge(w_pool_done, after(w_pool_steps, 0, "one_hot"))
                for m in range(NB):
                    if m >= 2:
                        pt.wait_ge(w_dve_done, after(w_dve_steps, 0, "picked", m - 2))
                    products(w_bank[1 + m % 2][:, 0:E], [(adj_sb[:, a, block_of(m)], raw(one_src[:, a, :]))
                                                         for a in range(NB)]).then_inc(w_pe_done, 1)
                pt.wait_ge(w_dve_done, after(w_dve_steps, 0, "picked", NB - 1))
                products(w_bank[3][0:1, 0:E], [(ones[:, 0:1], picked[:, m, :])
                                               for m in range(NB)]).then_inc(w_pe_done, 1)

            def w_soft():
                for a in range(NB):
                    if a >= 2:
                        pt.wait_ge(w_dve_done, after(w_dve_steps, 0, "rowmax", a - 2))
                    products(w_bank[a % 2][:, :], [(nv1_t[:, block_of(a)], nv2)]).then_inc(w_pe_done, 1)

            def scaled(factor):
                return ident_by[factor] if factor == 1.0 else raw(ident_by[factor])

            def w_q():
                pt.wait_ge(w_pool_done, after(w_pool_steps, 0, "q"))
                pt.wait_ge(w_dve_done, after(w_dve_steps, 0, "t_sum", NB - 1))
                for i in range(LOTS):
                    for place in range(LOT):
                        k = EULER_STEPS - i * LOT - place
                        (_, f_factor), *parts = q_parts[k]
                        p = EULER_STEPS - k
                        f_power = last_power if p == EULER_STEPS else power(p, 0)
                        last = products(w_bank[i][:, block_of(place)],
                                        [(f_power, scaled(f_factor))]
                                        + [(power(j - k, 1), scaled(factor)) for j, factor in parts])
                    last.then_inc(w_pe_done, 1)
                pt.wait_ge(w_dve_done, after(w_dve_steps, 0, "done"))

            def begin(turn, s, stage, i, *needs):
                if bank_user[stage, i] is not None:
                    old, j = bank_user[stage, i]
                    done, steps, what = last_reader[old]
                    needs += ((done, steps, what, 2 if old == "score" else j),)
                for done, steps in ((act_done, act_steps), (dve_done, dve_steps), (pool_done, pool_steps)):
                    values = [after(steps, 0, what, j) for d, _, what, j in needs if d is done]
                    if values:
                        pt.wait_ge(done[s], turn * len(steps) + max(values))

            def chunk(turn, s, stage, i, terms, out_=None, needs=()):
                begin(turn, s, stage, i, *needs)
                products(bank[s][i % 4][:, :] if out_ is None else out_, terms).then_inc(pe_done[s], 1)

            def transposes(turn, s, stage, b, *needs):
                begin(turn, s, stage, b, *needs)
                for a in range(NB):
                    last = T.transpose(bank[s][b][:, block_of(a)], X[s][:, a, b, :], ident[:, :])
                last.then_inc(pe_done[s], 1)

            def by_b(turn, s, stage, hi_step, lo_step, n, operands):
                done, steps, lo_what = lo_step
                for a in range(4):
                    i = 0 if n == NB else n - 1
                    begin(turn, s, stage, a, (act_done, act_steps, hi_step, i), lo_step + (i,))
                    T.matmul(bank[s][a][:, :], *operands(a, 0, BTH, ZH), start=True, stop=False)
                with pt.If(has_low != 0):
                    pt.wait_ge(act_done[s], after(act_steps, turn, hi_step, n - 1))
                    for a in range(4):
                        for m in range(NB):
                            T.matmul(bank[s][a][:, :], *operands(a, m, BTL, ZH), start=False, stop=False)
                for a in range(4):
                    for m in range(NB):
                        if n == NB and a == 0 and m > 0:
                            pt.wait_ge(act_done[s], after(act_steps, turn, hi_step, m))
                            pt.wait_ge(done[s], after(steps, turn, lo_what, m))
                        if m > 0:
                            T.matmul(bank[s][a][:, :], *operands(a, m, BTH, ZH), start=False, stop=False)
                        last = T.matmul(bank[s][a][:, :], *operands(a, m, BTH, ZL), start=False,
                                        stop=m == NB - 1)
                    last.then_inc(pe_done[s], 1)

            def left(s):
                return lambda a, m, b_t, z: (b_t[:, m, block_of(a)], z[s][:, m, :, :])

            def right(s):
                return lambda a, m, b_t, z: (z[s][:, m, a, :], b_t[:, m, :])

            def normalized(n, b):
                return ((act_done, act_steps, f"x{n}", b * NB + NB - 1) if b < GB // 2 else
                        (dve_done, dve_steps, f"x{n}", (b - GB // 2) * NB + NB - 1))

            def t0(turn, s):
                pt.wait_ge(x_loaded[s], (turn + 1) * (16 * NB))
                for b in range(GB):
                    transposes(turn, s, "t0", b)

            def neigh1(turn, s):
                by_b(turn, s, "neigh1", "x0_hi", (pool_done, pool_steps, "x0_lo"), NB, right(s))

            def conv1(turn, s):
                for b in range(GB):
                    chunk(turn, s, "conv1", b,
                          three(w1H[:, 0, :], w1L[:, 0, :], ZH[s][:, :, b, :], ZL[s][:, :, b, :])
                          + three(w1H[:, 1, :], w1L[:, 1, :], TH[s][:, b, :], TL[s][:, b, :]),
                          needs=((act_done, act_steps, "neigh1_hi", b), (pool_done, pool_steps, "neigh1_lo", b),
                                 (act_done, act_steps, "t0_hi", b), (dve_done, dve_steps, "t0_lo", b)))

            def pair2(turn, s):
                for i in range(8):
                    a, pair = i % 4, i // 4
                    begin(turn, s, "pair2", i, (act_done, act_steps, "h1_hi", 2 * pair + 1),
                          (pool_done, pool_steps, "h1_lo", 2 * pair + 1))
                    for c in range(2):
                        b = 2 * pair + c
                        last = products(bank[s][i % 4][:, block_of(c, 2 * D)],
                                        three(TH[s][:, b, block_of(a)], TL[s][:, b, block_of(a)],
                                              w2H[:, :], w2L[:, :]))
                    last.then_inc(pe_done[s], 1)

            def neigh2(turn, s):
                by_b(turn, s, "neigh2", "z2_hi", (dve_done, dve_steps, "z2_lo"), 8, left(s))

            def t1(turn, s):
                for b in range(GB):
                    transposes(turn, s, "t1", b, normalized(0, b))

            def lot(turn, s, l, a):
                part = slice(l * LOT, (l + 1) * LOT)
                for b in range(GB):
                    i = a * GB + b
                    chunk(turn, s, f"lot{l}", i, three(TH[s][:, b, block_of(a)], TL[s][:, b, block_of(a)],
                                                       QH[:, part, :], QL[:, part, :]),
                          bank[s][i % 4][:, 0:LOT * D],
                          ((act_done, act_steps, "t1_hi", b), (dve_done, dve_steps, "t1_lo", b)))

            def euler(turn, s, k):
                by_b(turn, s, f"euler{k}", f"euler{k + 1}_hi", (pool_done, pool_steps, f"euler{k + 1}_lo"), NB,
                     left(s))

            def t2(turn, s):
                for b in range(GB):
                    transposes(turn, s, "t2", b, normalized(1, b))

            def l2(turn, s, a):
                for i in range(2 * GB * a, 2 * GB * (a + 1)):
                    b, j = i // 2 % GB, i % 2
                    part = (slice(0, 3), slice(3, 5))[j]
                    chunk(turn, s, "l2", i, three(TH[s][:, b, block_of(a)], TL[s][:, b, block_of(a)],
                                                  VH[:, part, :], VL[:, part, :]),
                          bank[s][i % 4][:, 0:(3, 2)[j] * D],
                          ((act_done, act_steps, "t2_hi", b), (dve_done, dve_steps, "t2_lo", b)))

            def gather(turn, s):
                pt.wait_ge(act_done[s], after(act_steps, turn, "x3_hi", NB - 1))
                pt.wait_ge(pool_done[s], after(pool_steps, turn, "x3_lo", NB // 2 - 1))
                pt.wait_ge(dve_done[s], after(dve_steps, turn, "x3_lo", NB // 2 - 1))
                for b in range(GB):
                    chunk(turn, s, "gather", b, [(z[s][:, m, b, :], E1[:, m, :])
                                                 for m in range(NB) for z in (ZH, ZL)])

            def qv(turn, s):
                for b in range(GB):
                    begin(turn, s, "qv", b, (act_done, act_steps, "gather_hi", b),
                          (dve_done, dve_steps, "gather_lo", b))
                    for side in range(2):
                        part = block_of(side, E)
                        last = products(bank[s][b][:, part], three(gH[:, side, :], gL[:, side, :],
                                                                   TH[s][:, b, part], TL[s][:, b, part]))
                    last.then_inc(pe_done[s], 1)

            def score(turn, s):
                lo = HR - HEADS
                chunk(turn, s, "score", 0, [(a_pad[:, lo - HEADS * b:lo - HEADS * b + HR], l3(s, 1, b))
                                            for b in range(GB)] + [(ones[0:1, 0:HR], log_a[:, :])],
                      bank[s][0][0:HR, 0:E], ((dve_done, dve_steps, "leaky", GB - 1),))

            def spread(turn, s):
                for b in range(GB):
                    chunk(turn, s, "spread", b, [(head_of[:, b, :], seg(s, 7))], bank[s][b][:, 0:E],
                          ((dve_done, dve_steps, "seg", 6),))

            def wout(turn, s):
                for b in range(GB):
                    begin(turn, s, "wout", b, (dve_done, dve_steps, "mix", b))
                    for e in range(EB):
                        last = products(bank[s][b][:, block_of(e)], [(l3(s, 3, b)[:, block_of(e)], w_out[:, :])])
                    last.then_inc(pe_done[s], 1)

            def scatter(turn, s):
                for a in range(NB):
                    chunk(turn, s, "scatter", a, [(S1[:, e, block_of(a)], z[s][:, e, :, :])
                                                  for e in range(EB) for z in (ZH, ZL)],
                          needs=((act_done, act_steps, "wout_hi", GB - 1), (dve_done, dve_steps, "wout_lo", GB - 1)))

            stages = {"adj": w_adj, "low": w_low, "w0": w_w0, "v": w_v, "edges": w_edges, "powers": w_powers,
                      "l2_mean": w_l2,
                      "weights": w_weights, "picked": w_picked, "soft": w_soft, "end": w_q,
                      "t0": t0, "neigh1": neigh1, "conv1": conv1, "pair2": pair2, "neigh2": neigh2, "t1": t1,
                      "lot": lot, "euler": euler, "t2": t2, "l2": l2, "gather": gather, "qv": qv,
                      "score": score, "spread": spread, "wout": wout, "scatter": scatter}
            run(stages, prepare, 0)
            with pt.Fori(0, TURNS - 1) as turn:
                run(stages, in_turn, turn)
            run(stages, last_turn, TURNS - 1)


NAMES = ["x", "adj", "L0_gnn_w1_loop", "L0_gnn_w1_neigh", "L0_gnn_b1", "L0_gnn_w2_loop", "L0_gnn_w2_neigh",
         "L0_gnn_b2", "L1_gnn_alpha_train", "L1_gnn_w", "L1_gnn_d", "L1_gnn_fc_in_w", "L1_gnn_fc_in_b",
         "L2_gnn_node_vec1", "L2_gnn_node_vec2", "L2_gnn_W", "L2_gnn_b", "L3_gnn_W_lin", "L3_gnn_W_val",
         "L3_gnn_a", "L3_gnn_W_out", "L3_gnn_src", "L3_gnn_dst"]


def kernel(**inputs):
    import numpy as np
    import concourse.bacc as bacc
    from concourse.bass_utils import run_bass_kernel_spmd

    nc = bacc.Bacc("TRN2", target_bir_lowering=False, num_devices=1)
    arrays, tensors = {}, {}
    for name in NAMES:
        a = np.ascontiguousarray(inputs[name])
        arrays[f"in_{name}"] = a
        tensors[name] = nc.dram_tensor(f"in_{name}", a.shape, mybir.dt.from_np(a.dtype), kind="ExternalInput").ap()
    out = nc.dram_tensor("out_x", arrays["in_x"].shape, F32, kind="ExternalOutput").ap()
    build_program(nc, tensors, out)
    result = run_bass_kernel_spmd(nc, [arrays], core_ids=[0])
    return result.results[0]["out_x"]
```
